# Optimizing a Trainium2 kernel written in Bass

```python
import numpy as np
import jax
import jax.numpy as jnp

def _softmax(x, axis=-1):
    return jax.nn.softmax(x, axis=axis)

def _gelu(x):
    return jax.nn.gelu(x, approximate=True)

def _silu(x):
    return jax.nn.silu(x)

def _sigmoid(x):
    return jax.nn.sigmoid(x)

def _layernorm(x, axis=-1, eps=1e-05):
    m = jnp.mean(x, axis=axis, keepdims=True)
    v = jnp.var(x, axis=axis, keepdims=True)
    return (x - m) / jnp.sqrt(v + eps)

def _scatter_add(tgt, idx, src, axis=0):
    return tgt.at[idx].add(src)

def _segment_sum(src, seg, n):
    return jax.ops.segment_sum(src, seg, n)
kernel_name = 'mk_gnn_resnorm_d4_gnn_r32_adcf17'

def setup_inputs(seed: int=0):
    np.random.seed(seed)
    _w = jnp.asarray

    def _rec_inputs():
        import jax
        import jax.numpy as jnp
        _gk = jax.random.key(seed)
        x = -0.000202 + 1 * jax.random.normal(jax.random.fold_in(_gk, 1), (50000, 128), jnp.float32)
        src = jax.random.randint(jax.random.fold_in(_gk, 2), (25000,), 0, 50000, jnp.int32)
        dst = jnp.minimum((50000 * jax.random.uniform(jax.random.fold_in(_gk, 3), (25000,)) ** 2.0).astype(jnp.int32), 49999)
        _o = jnp.argsort(dst, stable=True)
        src = src[_o]
        dst = dst[_o]
        edge_attr_32 = 0.000196303 + 1.00016 * jax.random.normal(jax.random.fold_in(_gk, 11), (25000, 32), jnp.float32)
        edge_attr_64 = 0.000133148 + 1.00009 * jax.random.normal(jax.random.fold_in(_gk, 12), (25000, 64), jnp.float32)
        edge_weight = jax.random.uniform(jax.random.fold_in(_gk, 14), (25000,), jnp.float32, 0.0, 0.999999)
        return (x, src, dst, edge_attr_32, edge_attr_64, edge_weight)
    x, src, dst, edge_attr_32, edge_attr_64, edge_weight = _rec_inputs()

    def _L0_gnn_setup():
        import jax, jax.numpy as jnp
        import numpy as np
        N = 50000
        E = 18750
        D = 128
        H = 4
        C = D // H
        NEG_SLOPE = 0.2
        LN_EPS = 1e-05
        key = jax.random.key(seed)
        ks = jax.random.split(key, 6)
        s = 1.0 / np.sqrt(D)
        x = jax.random.normal(ks[0], (N, D), jnp.float32)
        edge_index = jax.random.randint(ks[1], (2, E), 0, N, dtype=jnp.int64)
        W = jax.random.normal(ks[2], (D, H * C), jnp.float32) * s
        att_src = jax.random.normal(ks[3], (H, C), jnp.float32) * s
        att_dst = jax.random.normal(ks[4], (H, C), jnp.float32) * s
        bias = jnp.zeros((H * C,), jnp.float32)
        gamma = jnp.ones((D,), jnp.float32)
        beta = jnp.zeros((D,), jnp.float32)
        return {'x': x, 'edge_index': edge_index, 'W': W, 'att_src': att_src, 'att_dst': att_dst, 'bias': bias, 'gamma': gamma, 'beta': beta}
    _L0_gnn_all = _L0_gnn_setup()
    _L0_gnn_in = {k: v for k, v in _L0_gnn_all.items() if k in ('W', 'att_src', 'att_dst', 'bias', 'gamma', 'beta')}
    del _L0_gnn_all

    def _L1_gnn_setup():
        import jax, jax.numpy as jnp
        import numpy as np
        N_NODES = 625
        N_EDGES = 20000
        NODE_DIM = 128
        HIDDEN = 128
        NUM_LAYERS = 3
        key = jax.random.key(seed)
        ks = jax.random.split(key, 6)
        x = jax.random.normal(ks[0], (N_NODES, NODE_DIM), dtype=jnp.float32)
        edge_index = jax.random.randint(ks[1], (2, N_EDGES), 0, N_NODES, dtype=jnp.int64)
        s = 1.0 / np.sqrt(NODE_DIM)
        W_in = jax.random.uniform(ks[2], (NODE_DIM, HIDDEN), jnp.float32, -s, s)
        b_in = jax.random.uniform(ks[3], (HIDDEN,), jnp.float32, -s, s)
        sh = 1.0 / np.sqrt(HIDDEN)
        Ws = jax.random.uniform(ks[4], (NUM_LAYERS, HIDDEN, HIDDEN), jnp.float32, -sh, sh)
        bs = jax.random.uniform(ks[5], (NUM_LAYERS, HIDDEN), jnp.float32, -sh, sh)
        return {'x': x, 'edge_index': edge_index, 'W_in': W_in, 'b_in': b_in, 'Ws': Ws, 'bs': bs}
    _L1_gnn_all = _L1_gnn_setup()
    _L1_gnn_in = {k: v for k, v in _L1_gnn_all.items() if k in ('W_in', 'b_in', 'Ws', 'bs')}
    del _L1_gnn_all

    def _L2_gnn_setup():
        import jax, jax.numpy as jnp
        import numpy as np
        import math
        N_NODES = 50000
        N_EDGES = 25000
        D = 128
        H = 8
        HD = D // H
        ED = 32
        key = jax.random.key(seed)
        ks = jax.random.split(key, 16)
        s = 1.0 / math.sqrt(D)
        se = 1.0 / math.sqrt(ED)
        return {'x': jax.random.normal(ks[0], (N_NODES, D), jnp.float32), 'edge_index': jax.random.randint(ks[1], (2, N_EDGES), 0, N_NODES, jnp.int64), 'edge_attr': jax.random.normal(ks[2], (N_EDGES, ED), jnp.float32), 'Wq': jax.random.normal(ks[3], (D, D), jnp.float32) * s, 'bq': jnp.zeros((D,), jnp.float32), 'Wk': jax.random.normal(ks[4], (D, D), jnp.float32) * s, 'bk': jnp.zeros((D,), jnp.float32), 'Wv': jax.random.normal(ks[5], (D, D), jnp.float32) * s, 'bv': jnp.zeros((D,), jnp.float32), 'We': jax.random.normal(ks[6], (ED, H), jnp.float32) * se, 'be': jnp.zeros((H,), jnp.float32), 'Wo': jax.random.normal(ks[7], (D, D), jnp.float32) * s, 'bo': jnp.zeros((D,), jnp.float32), 'gamma': jnp.ones((D,), jnp.float32), 'beta': jnp.zeros((D,), jnp.float32)}
    _L2_gnn_all = _L2_gnn_setup()
    _L2_gnn_in = {k: v for k, v in _L2_gnn_all.items() if k in ('Wq', 'bq', 'Wk', 'bk', 'Wv', 'bv', 'We', 'be', 'Wo', 'bo', 'gamma', 'beta')}
    del _L2_gnn_all

    def _L3_gnn_setup():
        import jax, jax.numpy as jnp
        import numpy as np
        N = 3125
        E = 50000
        IN = 128
        H = 4
        C = 32
        ED = 64

        def _forward(x, edge_weight, edge_attr, Wq, Wk, Wv, We, gate, bias, src, dst):
            n = x.shape[0]
            q_s = (x @ Wq).reshape(n, H, C).sum(-1)
            k_s = (x @ Wk).reshape(n, H, C).sum(-1)
            v = (x @ Wv).reshape(n, H, C)
            e_s = edge_attr @ We.reshape(ED, H, C).sum(-1)
            inv_sqrt_c = 1.0 / jnp.sqrt(jnp.asarray(C, x.dtype))
            alpha = (q_s[dst] + k_s[src] + e_s) * inv_sqrt_c
            alpha = alpha + gate[None, :] * edge_weight[:, None]
            alpha = jnp.where(alpha >= 0, alpha, 0.2 * alpha)
            amax = jax.ops.segment_max(alpha, dst, num_segments=n)
            amax = jnp.where(jnp.isfinite(amax), amax, 0.0)
            ex = jnp.exp(alpha - amax[dst])
            denom = jax.ops.segment_sum(ex, dst, num_segments=n)
            attn = ex / (denom[dst] + 1e-16)
            msg = v[src] * attn[:, :, None]
            out = jax.ops.segment_sum(msg, dst, num_segments=n)
            return out.reshape(n, H * C) + bias
        key = jax.random.key(seed)
        ks = jax.random.split(key, 9)
        x = jax.random.normal(ks[0], (N, IN), jnp.float32)
        edge_index = jax.random.randint(ks[1], (2, E), 0, N, dtype=jnp.int32)
        edge_weight = jax.random.uniform(ks[2], (E,), jnp.float32)
        edge_attr = jax.random.normal(ks[3], (E, ED), jnp.float32)
        sq = float(np.sqrt(2.0 / (IN + H * C)))
        se = float(np.sqrt(2.0 / (ED + H * C)))
        Wq = jax.random.normal(ks[4], (IN, H * C), jnp.float32) * sq
        Wk = jax.random.normal(ks[5], (IN, H * C), jnp.float32) * sq
        Wv = jax.random.normal(ks[6], (IN, H * C), jnp.float32) * sq
        We = jax.random.normal(ks[7], (ED, H * C), jnp.float32) * se
        gate = jnp.ones((H,), jnp.float32)
        bias = jnp.zeros((H * C,), jnp.float32)
        return {'x': x, 'edge_index': edge_index, 'edge_weight': edge_weight, 'edge_attr': edge_attr, 'Wq': Wq, 'Wk': Wk, 'Wv': Wv, 'We': We, 'gate': gate, 'bias': bias}
    _L3_gnn_all = _L3_gnn_setup()
    _L3_gnn_in = {k: v for k, v in _L3_gnn_all.items() if k in ('Wq', 'Wk', 'Wv', 'We', 'gate', 'bias')}
    del _L3_gnn_all
    return {'x': x, 'src': src, 'dst': dst, 'edge_attr_32': edge_attr_32, 'edge_attr_64': edge_attr_64, 'edge_weight': edge_weight, 'L0_gnn_W': _L0_gnn_in['W'], 'L0_gnn_att_src': _L0_gnn_in['att_src'], 'L0_gnn_att_dst': _L0_gnn_in['att_dst'], 'L0_gnn_bias': _L0_gnn_in['bias'], 'L0_gnn_gamma': _L0_gnn_in['gamma'], 'L0_gnn_beta': _L0_gnn_in['beta'], 'L1_gnn_W_in': _L1_gnn_in['W_in'], 'L1_gnn_b_in': _L1_gnn_in['b_in'], 'L1_gnn_Ws': _L1_gnn_in['Ws'], 'L1_gnn_bs': _L1_gnn_in['bs'], 'L2_gnn_Wq': _L2_gnn_in['Wq'], 'L2_gnn_bq': _L2_gnn_in['bq'], 'L2_gnn_Wk': _L2_gnn_in['Wk'], 'L2_gnn_bk': _L2_gnn_in['bk'], 'L2_gnn_Wv': _L2_gnn_in['Wv'], 'L2_gnn_bv': _L2_gnn_in['bv'], 'L2_gnn_We': _L2_gnn_in['We'], 'L2_gnn_be': _L2_gnn_in['be'], 'L2_gnn_Wo': _L2_gnn_in['Wo'], 'L2_gnn_bo': _L2_gnn_in['bo'], 'L2_gnn_gamma': _L2_gnn_in['gamma'], 'L2_gnn_beta': _L2_gnn_in['beta'], 'L3_gnn_Wq': _L3_gnn_in['Wq'], 'L3_gnn_Wk': _L3_gnn_in['Wk'], 'L3_gnn_Wv': _L3_gnn_in['Wv'], 'L3_gnn_We': _L3_gnn_in['We'], 'L3_gnn_gate': _L3_gnn_in['gate'], 'L3_gnn_bias': _L3_gnn_in['bias']}

def reference(x, src, dst, edge_attr_32, edge_attr_64, edge_weight, L0_gnn_W, L0_gnn_att_src, L0_gnn_att_dst, L0_gnn_bias, L0_gnn_gamma, L0_gnn_beta, L1_gnn_W_in, L1_gnn_b_in, L1_gnn_Ws, L1_gnn_bs, L2_gnn_Wq, L2_gnn_bq, L2_gnn_Wk, L2_gnn_bk, L2_gnn_Wv, L2_gnn_bv, L2_gnn_We, L2_gnn_be, L2_gnn_Wo, L2_gnn_bo, L2_gnn_gamma, L2_gnn_beta, L3_gnn_Wq, L3_gnn_Wk, L3_gnn_Wv, L3_gnn_We, L3_gnn_gate, L3_gnn_bias):
    import jax
    import jax.numpy as jnp

    def _L0_gnn_ref(x, edge_index, W, att_src, att_dst, bias, gamma, beta):
        import jax, jax.numpy as jnp
        import numpy as np
        N = 50000
        E = 18750
        D = 128
        H = 4
        C = D // H
        NEG_SLOPE = 0.2
        LN_EPS = 1e-05
        n = x.shape[0]
        h = (x @ W).reshape(n, H, C)
        loops = jnp.arange(n, dtype=edge_index.dtype)
        src = jnp.concatenate([edge_index[0], loops])
        dst = jnp.concatenate([edge_index[1], loops])
        a_src = jnp.einsum('nhc,hc->nh', h, att_src)
        a_dst = jnp.einsum('nhc,hc->nh', h, att_dst)
        e = jax.nn.leaky_relu(a_src[src] + a_dst[dst], NEG_SLOPE)
        m = jax.ops.segment_max(e, dst, num_segments=n)
        e = jnp.exp(e - m[dst])
        denom = jax.ops.segment_sum(e, dst, num_segments=n)
        alpha = e / (denom[dst] + 1e-16)
        msg = h[src] * alpha[:, :, None]
        out = jax.ops.segment_sum(msg, dst, num_segments=n).reshape(n, H * C) + bias
        f = jax.nn.gelu(out, approximate=False)
        mu = jnp.mean(f, axis=-1, keepdims=True)
        var = jnp.var(f, axis=-1, keepdims=True)
        f = (f - mu) / jnp.sqrt(var + LN_EPS) * gamma + beta
        return f + x

    def _L1_gnn_ref(x, edge_index, W_in, b_in, Ws, bs):
        import jax, jax.numpy as jnp
        import numpy as np
        N_NODES = 625
        N_EDGES = 20000
        NODE_DIM = 128
        HIDDEN = 128
        NUM_LAYERS = 3
        N = x.shape[0]
        loop = jnp.arange(N, dtype=edge_index.dtype)
        src = jnp.concatenate([edge_index[0], loop])
        dst = jnp.concatenate([edge_index[1], loop])
        deg = jax.ops.segment_sum(jnp.ones_like(dst, dtype=x.dtype), dst, num_segments=N)
        dis = jax.lax.rsqrt(jnp.where(deg > 0, deg, 1.0))
        norm = dis[src] * dis[dst]
        h = x @ W_in + b_in
        for i in range(Ws.shape[0]):
            xw = h @ Ws[i]
            msg = xw[src] * norm[:, None]
            agg = jax.ops.segment_sum(msg, dst, num_segments=N) + bs[i]
            h = jax.nn.relu(agg)
        return h

    def _L2_gnn_ref(x, edge_index, edge_attr, Wq, bq, Wk, bk, Wv, bv, We, be, Wo, bo, gamma, beta):
        import jax, jax.numpy as jnp
        import numpy as np
        import math
        N_NODES = 50000
        N_EDGES = 25000
        D = 128
        H = 8
        HD = D // H
        ED = 32
        n = x.shape[0]
        residual = x
        q = (x @ Wq + bq).reshape(n, H, HD)
        k = (x @ Wk + bk).reshape(n, H, HD)
        v = (x @ Wv + bv).reshape(n, H, HD)
        src = edge_index[0]
        dst = edge_index[1]
        score = jnp.einsum('ehd,ehd->eh', q[dst], k[src]) / math.sqrt(HD)
        score = score + edge_attr @ We + be
        m = jax.ops.segment_max(score, dst, num_segments=n)
        exp_s = jnp.exp(score - m[dst])
        ssum = jax.ops.segment_sum(exp_s, dst, num_segments=n)
        attn = exp_s / (ssum[dst] + 1e-08)
        msg = attn[..., None] * v[src]
        out = jax.ops.segment_sum(msg, dst, num_segments=n)
        out = out.reshape(n, D) @ Wo + bo
        h = out + residual
        mu = h.mean(-1, keepdims=True)
        var = ((h - mu) ** 2).mean(-1, keepdims=True)
        return (h - mu) / jnp.sqrt(var + 1e-05) * gamma + beta

    def _L3_gnn_ref(x, edge_index, edge_weight, edge_attr, Wq, Wk, Wv, We, gate, bias):
        import jax, jax.numpy as jnp
        import numpy as np
        N = 3125
        E = 50000
        IN = 128
        H = 4
        C = 32
        ED = 64

        def _forward(x, edge_weight, edge_attr, Wq, Wk, Wv, We, gate, bias, src, dst):
            n = x.shape[0]
            q_s = (x @ Wq).reshape(n, H, C).sum(-1)
            k_s = (x @ Wk).reshape(n, H, C).sum(-1)
            v = (x @ Wv).reshape(n, H, C)
            e_s = edge_attr @ We.reshape(ED, H, C).sum(-1)
            inv_sqrt_c = 1.0 / jnp.sqrt(jnp.asarray(C, x.dtype))
            alpha = (q_s[dst] + k_s[src] + e_s) * inv_sqrt_c
            alpha = alpha + gate[None, :] * edge_weight[:, None]
            alpha = jnp.where(alpha >= 0, alpha, 0.2 * alpha)
            amax = jax.ops.segment_max(alpha, dst, num_segments=n)
            amax = jnp.where(jnp.isfinite(amax), amax, 0.0)
            ex = jnp.exp(alpha - amax[dst])
            denom = jax.ops.segment_sum(ex, dst, num_segments=n)
            attn = ex / (denom[dst] + 1e-16)
            msg = v[src] * attn[:, :, None]
            out = jax.ops.segment_sum(msg, dst, num_segments=n)
            return out.reshape(n, H * C) + bias
        src, dst = (edge_index[0], edge_index[1])
        return _forward(x, edge_weight, edge_attr, Wq, Wk, Wv, We, gate, bias, src, dst)
    edge_index = jnp.stack([src, dst])
    x = _layernorm(x + _L0_gnn_ref(x, edge_index, L0_gnn_W, L0_gnn_att_src, L0_gnn_att_dst, L0_gnn_bias, L0_gnn_gamma, L0_gnn_beta), axis=-1)
    x = _layernorm(x + _L1_gnn_ref(x, edge_index, L1_gnn_W_in, L1_gnn_b_in, L1_gnn_Ws, L1_gnn_bs), axis=-1)
    x = _layernorm(x + _L2_gnn_ref(x, edge_index, edge_attr_32, L2_gnn_Wq, L2_gnn_bq, L2_gnn_Wk, L2_gnn_bk, L2_gnn_Wv, L2_gnn_bv, L2_gnn_We, L2_gnn_be, L2_gnn_Wo, L2_gnn_bo, L2_gnn_gamma, L2_gnn_beta), axis=-1)
    x = _layernorm(x + _L3_gnn_ref(x, edge_index, edge_weight, edge_attr_64, L3_gnn_Wq, L3_gnn_Wk, L3_gnn_Wv, L3_gnn_We, L3_gnn_gate, L3_gnn_bias), axis=-1)
    return x

_drawn_inputs = setup_inputs


def setup_inputs(seed=0):
    import zlib

    import numpy as np

    out = dict(_drawn_inputs(seed))
    spreads = {'L0_gnn_bias': (0.0, 0.1),
     'L0_gnn_gamma': (1.0, 0.2),
     'L0_gnn_beta': (0.0, 0.1),
     'L2_gnn_bq': (0.0, 2.0),
     'L2_gnn_bk': (0.0, 2.0),
     'L2_gnn_bv': (0.0, 0.365),
     'L2_gnn_be': (0.0, 2.0),
     'L2_gnn_bo': (0.0, 0.1),
     'L2_gnn_gamma': (1.0, 0.2),
     'L2_gnn_beta': (0.0, 0.1),
     'L3_gnn_gate': (1.0, 0.6),
     'L3_gnn_bias': (0.0, 0.1)}
    factors = {'L0_gnn_att_dst': 2.708, 'L1_gnn_b_in': 8.0, 'L3_gnn_Wq': 2.899}
    for name, (base, spread) in spreads.items():
        noise = np.random.default_rng([zlib.crc32(name.encode()), seed]).standard_normal(out[name].shape)
        drawn = base * np.exp(spread * noise) if base else spread * noise
        out[name] = jnp.asarray(drawn.astype(out[name].dtype))
    for name, factor in factors.items():
        out[name] = (out[name] * factor).astype(out[name].dtype)
    return out
```

```python
from contextlib import ExitStack

import concourse.bass as bass
from concourse import mybir

F32 = mybir.dt.float32
I32 = mybir.dt.int32
U32 = mybir.dt.uint32
ALU = mybir.AluOpType
ACT = mybir.ActivationFunctionType
AX = mybir.AxisListType

P = 128
D = 128
SUB = 4
CH = P * SUB
NODES, EDGES = 50000, 25000
NL = 4
EL = 2
N_IT = -(-NODES // (CH * NL))
E_IT = -(-EDGES // (CH * EL))
NT = N_IT * NL * CH
ET = E_IT * EL * CH
TILES = ET // P
IT_TILES = EL * SUB
MAP_IT = (N_IT + 1) // 2
MAP_W = -(-TILES // MAP_IT)
READ_IT = N_IT - MAP_IT
MAP_R = -(-TILES // READ_IT)
COLS = max(MAP_W * MAP_IT, MAP_R * READ_IT, TILES + IT_TILES)
FAR = 1000000
BIG = 3.0e38
EPS = 1e-5


def build(nc, x, src, dst, ea32, ea64, ew, w, out):
    ctx = ExitStack()

    def sb(name, shape, dt=F32):
        return ctx.enter_context(nc.sbuf_tensor(name, shape, dt))

    def dram(name, shape, dt=F32):
        return nc.dram_tensor(name, shape, dt, kind="Internal").ap()

    sems, handles = {}, []

    def S(name):
        if name not in sems:
            if len(sems) == len(handles):
                handles.append(ctx.enter_context(nc.semaphore(f"signal_{len(handles)}")))
            sems[name] = handles[len(sems)]
        return sems[name]

    pool_dma = {n: ctx.enter_context(nc.semaphore(n)) for n in
                ("edges", "map_written", "map_read", "gathered_h0", "gathered_g0", "gathered_g1", "gathered_g2",
                 "gathered_t2", "gathered_t3", "scattered")}

    def new_phase():
        sems.clear()

    def all_meet():
        numbers = sorted(s.num for s in handles)
        assert numbers == list(range(numbers[0], numbers[0] + len(numbers)))
        nc.all_engine_barrier()
        nc.gpsimd.sem_clear(range(numbers[0], numbers[0] + len(numbers)))
        nc.all_engine_barrier()

    tables = [dram(f"table_{n}", [NT + ET, D]) for n in ("xw0", "xw1", "xw2", "x2", "x3")]
    x1_slots = dram("x1_slots", [ET, D])
    node_map = dram("node_map", [NT, 1], U32)
    pen_row = dram("pen_row", [1, ET])
    nst_row = dram("nst_row", [1, ET])
    cnt_row = dram("cnt_row", [1, ET])

    ident = sb("ident", [P, P])
    ones = sb("ones", [1, P])
    eps = sb("eps", [P, 1])
    W0 = sb("W0", [P, D])
    WI0 = sb("WI0", [P, D])
    WS = [None, sb("WS1", [P, D]), sb("WS2", [P, D])]
    src_rep, dst_rep, self_rep = (sb(n, [P, D]) for n in ("src_rep", "dst_rep", "self_rep"))
    xw0_bias_row = sb("xw0_bias_row", [1, D])
    h1_bias = sb("h1_bias", [P, 1])
    h2_bias = sb("h2_bias", [P, 1])
    bias0, gamma0, beta0 = (sb(n, [P, D]) for n in ("bias0", "gamma0", "beta0"))
    bs_row = [sb(f"bs_row{i}", [P, D]) for i in range(3)]
    Wq, Wk, Wv, Wo = (sb(n, [P, D]) for n in ("Wq", "Wk", "Wv", "Wo"))
    bq, bk, bv = (sb(n, [P, 1]) for n in ("bq", "bk", "bv"))
    bo, gamma2, beta2 = (sb(n, [P, D]) for n in ("bo", "gamma2", "beta2"))
    we2_rep = sb("we2_rep", [33, D])
    head_sum = sb("head_sum", [P, D])
    q3_rep, k3_rep, Wv3 = (sb(n, [P, D]) for n in ("q3_rep", "k3_rep", "Wv3"))
    we3_rep = sb("we3_rep", [65, D])
    bias3 = sb("bias3", [P, D])
    sel4, sel8 = sb("sel4", [P, 4]), sb("sel8", [P, 8])
    src_idx = sb("src_idx", [P, COLS], U32)
    dst_idx = sb("dst_idx", [P, COLS], U32)
    end_idx = sb("end_idx", [P, COLS], U32)
    slot_idx = sb("slot_idx", [P, COLS], U32)
    own_idx = sb("own_idx", [P, COLS], U32)
    slot_no = sb("slot_no", [P, COLS], U32)
    dis = sb("dis", [P, COLS])

    ps = ctx.enter_context(nc.psum_tensor("ps", [P, 8, CH], F32))

    def rows4(t):
        return t.rearrange("p (j f) -> p j f", j=SUB)

    def each_row(row):
        return row[:, None, :].to_broadcast([P, SUB, D])

    def by_row(cols, width=D):
        return cols[:, :, None].to_broadcast([P, cols.shape[1], width])

    with ExitStack() as tmp:
        def tb(name, shape, dt=F32):
            return tmp.enter_context(nc.sbuf_tensor(name, shape, dt))

        H = TILES // 2
        edge_i = tb("edge_i", [H, 2, 4, P], I32)
        edge_f = tb("edge_f", [H, 2, 4, P])
        mark = tb("mark", [H, 2, 5, P])
        att = tb("att", [P, 2, D])
        prod = tb("prod", [P, 4, D])
        sums = tb("sums", [P, 6, 4])
        Win, WinT, Ws0 = tb("Win", [P, D]), tb("WinT", [P, D]), tb("Ws0", [P, D])
        b_in, bs0c = tb("b_in", [P, 1]), tb("bs0c", [P, 1])
        We2, We3 = tb("We2", [33, 8]), tb("We3", [64, D])
        We3s = tb("We3s", [65, 4])
        Wq3, Wk3 = tb("Wq3", [P, D]), tb("Wk3", [P, D])
        node_no = tb("node_no", [P, NT // P], U32)
        cnt_in = tb("cnt_in", [1, ET // 8])
        cnt_out = tb("cnt_out", [1, ET // 8])
        one_row = tb("one_row", [1, ET // 8])
        cnt_last = tb("cnt_last", [1, 1])
        deg_rows = tb("deg_rows", [H, 2, P])
        deg = tb("deg", [P, TILES])

        cols = [(b_in, w["L1_gnn_b_in"]), (bs0c, w["L1_gnn_bs"][0]), (h2_bias, w["L1_gnn_bs"][1]),
                (bq, w["L2_gnn_bq"]), (bk, w["L2_gnn_bk"]), (bv, w["L2_gnn_bv"])]
        rows = [(bias0, w["L0_gnn_bias"]), (gamma0, w["L0_gnn_gamma"]), (beta0, w["L0_gnn_beta"]),
                (bs_row[0], w["L1_gnn_bs"][0]), (bs_row[1], w["L1_gnn_bs"][1]),
                (bs_row[2], w["L1_gnn_bs"][2]), (bo, w["L2_gnn_bo"]),
                (gamma2, w["L2_gnn_gamma"]), (beta2, w["L2_gnn_beta"]), (bias3, w["L3_gnn_bias"]),
                (att[:, 0, :], w["L0_gnn_att_src"].rearrange("h c -> (h c)")),
                (att[:, 1, :], w["L0_gnn_att_dst"].rearrange("h c -> (h c)"))]
        mats = [(W0, w["L0_gnn_W"]), (Win, w["L1_gnn_W_in"]), (Ws0, w["L1_gnn_Ws"][0]),
                (WS[1], w["L1_gnn_Ws"][1]), (WS[2], w["L1_gnn_Ws"][2]),
                (Wq, w["L2_gnn_Wq"]), (Wk, w["L2_gnn_Wk"]), (Wv, w["L2_gnn_Wv"]), (Wo, w["L2_gnn_Wo"]),
                (Wv3, w["L3_gnn_Wv"]), (Wq3, w["L3_gnn_Wq"]), (Wk3, w["L3_gnn_Wk"]),
                (We3, w["L3_gnn_We"])]
        small = [(We2[0:32, :], w["L2_gnn_We"]), (We2[32:33, :], w["L2_gnn_be"][None, :]),
                 (We3s[64:65, :], w["L3_gnn_gate"][None, :])]
        loads = ([(c[:], a.rearrange("(p o) -> p o", o=1)) for c, a in cols]
                 + [(r[:, :], a[None, :].to_broadcast([P, D])) for r, a in rows]
                 + [(m[:], a) for m, a in mats] + small)
        edge_loads = [(edge_i[:, :, 0, :], src.rearrange("(h r c) -> r h c", h=2, c=P))] + [
            (edge_i[:, :, k, :], dst[o:o + ET].rearrange("(h r c) -> r h c", h=2, c=P))
            for k, o in ((1, 1), (2, 0), (3, 2))]

        with nc.Block() as block:
            @block.sync
            def _(sp):
                for to, of in loads:
                    sp.dma_start(to, of).then_inc(S("weights"), 16)
                sp.wait_ge(S("node_no"), 1)
                sp.dma_start(node_map.rearrange("(p c) o -> p (c o)", p=P), node_no[:]).then_inc(S("stored"), 16)
                sp.wait_ge(S("marks"), 2)
                for row, k in ((nst_row, 1), (pen_row, 2)):
                    sp.dma_start(row.rearrange("o (h r c) -> (o r) h c", h=2, c=P), mark[:, :, k, :]).then_inc(S("rows_stored"), 16)
                sp.wait_ge(S("rows_stored"), 32)
                for k in range(8):
                    if k:
                        sp.wait_ge(S("counted"), k)
                    piece = slice(k * (ET // 8), (k + 1) * (ET // 8))
                    sp.dma_start(cnt_in[:], nst_row[:, piece]).then_inc(S("cnt_loaded"), 16)
                    sp.wait_ge(S("counted"), k + 1)
                    sp.dma_start(cnt_row[:, piece], cnt_out[:]).then_inc(S("cnt_stored"), 16)
                    sp.wait_ge(S("cnt_stored"), 16 * (k + 1))
                sp.dma_start(deg_rows[:], cnt_row.rearrange("o (h r c) -> (o r) h c", h=2, c=P)).then_inc(S("deg_rows"), 16)
                sp.wait_ge(S("stored"), 16)

            @block.gpsimd
            def _(pool):
                for to, of in edge_loads:
                    pool.dma_start(to, of).then_inc(pool_dma["edges"], 16)
                nc.gpsimd.iota(node_no[:], pattern=[[1, NT // P]], base=0, channel_multiplier=NT // P).then_inc(S("node_no"), 1)
                nc.gpsimd.iota(slot_no[:], pattern=[[P, COLS]], base=NT, channel_multiplier=1).then_inc(S("slot_no"), 1)
                nc.gpsimd.memset(src_idx[:], 0).then_inc(S("zeros"), 1)
                nc.gpsimd.memset(dst_idx[:], 0).then_inc(S("zeros"), 1)
                nc.gpsimd.memset(end_idx[:], FAR).then_inc(S("zeros"), 1)
                nc.gpsimd.memset(slot_idx[:], 0).then_inc(S("zeros"), 1)
                nc.gpsimd.memset(own_idx[:], 0).then_inc(S("zeros"), 1)
                nc.gpsimd.memset(dis[:], 0.0).then_inc(S("zeros"), 1)
                nc.gpsimd.memset(ones[:], 1.0).then_inc(S("zeros"), 1)
                nc.gpsimd.memset(eps[:], EPS).then_inc(S("zeros"), 1)
                for t in (ident, sel4, sel8):
                    nc.gpsimd.memset(t[:], 0.0).then_inc(S("cleared"), 1)
                nc.gpsimd.memset(head_sum[:], 0.25).then_inc(S("cleared"), 1)
                pool.wait_ge(S("cleared"), 4)
                for t, n in ((ident, 1), (sel4, 32), (sel8, 16)):
                    nc.gpsimd.affine_select(out=t[:], in_=t[:], compare_op=ALU.not_equal, fill=1.0, base=0,
                                            pattern=[[-n, t.shape[1]]], channel_multiplier=1).then_inc(S("masks"), 1)
                hs = head_sum.rearrange("p (h c) -> p h c", h=8)
                nc.gpsimd.affine_select(out=hs, in_=hs, compare_op=ALU.is_ge, fill=0.0, base=0,
                                        pattern=[[-16, 8], [0, 16]], channel_multiplier=1).then_inc(S("masks"), 1)
                pool.wait_ge(S("masks"), 4)
                nc.gpsimd.affine_select(out=hs, in_=hs, compare_op=ALU.is_ge, fill=0.0, base=15,
                                        pattern=[[16, 8], [0, 16]], channel_multiplier=-1).then_inc(S("masks"), 1)

            @block.tensor
            def _(pe):
                pe.wait_ge(S("masks"), 5)
                pe.wait_ge(S("zeros"), 8)
                pe.wait_ge(S("weights"), 16 * len(loads))
                nc.tensor.transpose(ps[:, 0, 0:P], Win[:], ident[:]).then_inc(S("win_ps"), 1)
                pe.wait_ge(S("winT"), 1)
                nc.tensor.matmul(ps[:, 0, 128:256], WinT[:], Ws0[:], start=True, stop=True).then_inc(S("wi0_ps"), 1)
                nc.tensor.matmul(ps[0:1, 0, 256:384], b_in[:], Ws0[:], start=True, stop=True).then_inc(S("wi0_ps"), 1)
                nc.tensor.matmul(ps[:, 0, 384:385], Ws0[:], b_in[:], start=True, stop=True).then_inc(S("wi0_ps"), 1)
                pe.wait_ge(S("marks"), 2)
                for h in range(2):
                    for k, t in enumerate((edge_f[:, h, 0, :], edge_f[:, h, 1, :], mark[:, h, 3, :])):
                        nc.tensor.transpose(ps[:, 1 + k, h * H:(h + 1) * H], t, ident[0:H, 0:H]).then_inc(S("cols_ps"), 1)
                pe.wait_ge(S("deg_rows"), 16)
                for h in range(2):
                    nc.tensor.transpose(ps[:, 4, h * H:(h + 1) * H], deg_rows[:, h, :], ident[0:H, 0:H]).then_inc(S("deg_ps"), 1)

            @block.scalar
            def _(act):
                act.wait_ge(S("deg_ps"), 2)
                nc.scalar.activation(deg[:], ps[:, 4, 0:TILES], ACT.Sqrt, bias=1.0).then_inc(S("deg"), 1)

            @block.vector
            def _(v):
                V = nc.vector
                v.wait_ge(pool_dma["edges"], 64)
                V.tensor_copy(edge_f[:], edge_i[:]).then_inc(S("edges_f"), 1)
                v.wait_ge(S("edges_f"), 1)
                V.tensor_tensor(mark[:, :, 0, :], edge_f[:, :, 1, :], edge_f[:, :, 3, :], ALU.is_equal).then_inc(S("m"), 1)
                V.tensor_tensor(mark[:, :, 1, :], edge_f[:, :, 1, :], edge_f[:, :, 2, :], ALU.is_equal).then_inc(S("m"), 1)
                v.wait_ge(S("m"), 2)
                V.tensor_scalar(mark[:, :, 4, :], mark[:, :, 0, :], float(FAR), None, ALU.mult).then_inc(S("m"), 1)
                V.tensor_scalar(mark[:, :, 2, :], mark[:, :, 1, :], 0.5, 2 * BIG / 2, ALU.subtract, ALU.mult).then_inc(S("marks"), 1)
                v.wait_ge(S("m"), 3)
                V.tensor_tensor(mark[:, :, 3, :], mark[:, :, 4, :], edge_f[:, :, 1, :], ALU.add).then_inc(S("marks"), 1)
                v.wait_ge(S("win_ps"), 1)
                V.tensor_copy(WinT[:], ps[:, 0, 0:P]).then_inc(S("winT"), 1)
                v.wait_ge(S("wi0_ps"), 3)
                V.tensor_copy(WI0[:], ps[:, 0, 128:256])
                V.tensor_copy(xw0_bias_row[:], ps[0:1, 0, 256:384])
                V.tensor_tensor(h1_bias[:], ps[:, 0, 384:385], bs0c[:], ALU.add)
                V.tensor_tensor(prod[:, 0, :], W0[:], att[:, 0, :], ALU.mult).then_inc(S("prod"), 1)
                V.tensor_tensor(prod[:, 1, :], W0[:], att[:, 1, :], ALU.mult).then_inc(S("prod"), 1)
                v.wait_ge(S("prod"), 2)
                for k, t in enumerate((prod[:, 0, :], prod[:, 1, :], Wq3[:], Wk3[:])):
                    V.tensor_reduce(sums[:, k, :], t.rearrange("p (h c) -> p h c", h=4), AX.X, ALU.add).then_inc(S("sums"), 1)
                V.tensor_reduce(We3s[0:64, :], We3[:].rearrange("p (h c) -> p h c", h=4), AX.X, ALU.add).then_inc(S("sums"), 1)
                v.wait_ge(S("sums"), 5)
                for k, t in enumerate((src_rep, dst_rep, q3_rep, k3_rep)):
                    V.tensor_copy(t.rearrange("p (h c) -> p h c", h=4), by_row(sums[:, k, :], 32)).then_inc(S("rep"), 1)
                V.tensor_copy(we3_rep[0:64, :].rearrange("p (h c) -> p h c", h=4),
                              We3s[0:64, :, None].to_broadcast([64, 4, 32]))
                V.tensor_scalar(we3_rep[64:65, :].rearrange("p (h c) -> p h c", h=4),
                                We3s[64:65, :, None].to_broadcast([1, 4, 32]), float(32.0 ** 0.5), None, ALU.mult)
                V.tensor_copy(we2_rep.rearrange("p (h c) -> p h c", h=8), We2[:, :, None].to_broadcast([33, 8, 16]))
                v.wait_ge(S("rep"), 4)
                V.tensor_tensor(self_rep[:], src_rep[:], dst_rep[:], ALU.add)
                v.wait_ge(S("cols_ps"), 6)
                v.wait_ge(S("zeros"), 8)
                V.tensor_copy(src_idx[:, 0:TILES], ps[:, 1, 0:TILES])
                V.tensor_copy(dst_idx[:, 0:TILES], ps[:, 2, 0:TILES])
                V.tensor_copy(end_idx[:, 0:TILES], ps[:, 3, 0:TILES])
                V.memset(one_row[:], 1.0).then_inc(S("cnt_init"), 1)
                V.memset(cnt_last[:], 0.0).then_inc(S("cnt_init"), 1)
                for k in range(8):
                    v.wait_ge(S("cnt_init"), 2 + k)
                    v.wait_ge(S("cnt_loaded"), 16 * (k + 1))
                    if k:
                        v.wait_ge(S("cnt_stored"), 16 * k)
                    V.tensor_tensor_scan(cnt_out[:], cnt_in[:], one_row[:], cnt_last[:], ALU.mult, ALU.add).then_inc(S("counted"), 1)
                    v.wait_ge(S("counted"), k + 1)
                    V.tensor_copy(cnt_last[:], cnt_out[:, ET // 8 - 1:ET // 8]).then_inc(S("cnt_init"), 1)
                v.wait_ge(S("deg"), 1)
                V.reciprocal(dis[:, 0:TILES], deg[:])
        all_meet()

    def ln_stats(v, n, L, b, t, ready):
        v.wait_ge(S(ready), L + 1)
        for j in range(SUB):
            nc.vector.bn_stats(b["st"][:, 6 * j:6 * j + 6], t[:, j * D:(j + 1) * D]).then_inc(S(n + "_st"), 1)
        v.wait_ge(S(n + "_st"), SUB * (L + 1))
        for j in range(SUB):
            nc.vector.bn_aggr(b["mv"][:, 2 * j:2 * j + 2], b["st"][:, 6 * j:6 * j + 6]).then_inc(S(n + "_mv"), 1)

    def ln_root(act, n, L, b):
        act.wait_ge(S(n + "_mv"), SUB * (L + 1))
        var = b["mv"].rearrange("p (j t) -> p j t", t=2)[:, :, 1]
        nc.scalar.activation(b["sd"][:], var, ACT.Sqrt, bias=eps[:, 0:1]).then_inc(S(n + "_sd"), 1)

    def ln_scale(v, n, L, b):
        v.wait_ge(S(n + "_sd"), L + 1)
        nc.vector.reciprocal(b["rs"][:], b["sd"][:]).then_inc(S(n + "_rs"), 1)
        v.wait_ge(S(n + "_rs"), L + 1)
        mean = b["mv"].rearrange("p (j t) -> p j t", t=2)[:, :, 0]
        nc.vector.scalar_tensor_tensor(out=b["nm"][:], in0=mean, scalar=-1.0, in1=b["rs"][:],
                                       op0=ALU.mult, op1=ALU.mult).then_inc(S(n + "_nm"), 1)

    def ln_apply(act, n, L, b, to, t):
        act.wait_ge(S(n + "_nm"), L + 1)
        for j in range(SUB):
            last = nc.scalar.activation(to[:, j * D:(j + 1) * D], t[:, j * D:(j + 1) * D], ACT.Identity,
                                        scale=b["rs"][:, j:j + 1], bias=b["nm"][:, j:j + 1])
        last.then_inc(S(n + "_out"), 1)

    def turn(pe, to, t, width=P):
        for j in range(SUB):
            last = nc.tensor.transpose(to[0:width, j * P:(j + 1) * P], t[:, j * width:(j + 1) * width], ident[:])
        return last

    def rows_times(pe, to, tT, W, bias_row=None):
        for j in range(SUB):
            last = nc.tensor.matmul(to[:, j * D:(j + 1) * D], tT[:, j * P:(j + 1) * P], W[:],
                                    start=True, stop=bias_row is None)
            if bias_row is not None:
                last = nc.tensor.matmul(to[:, j * D:(j + 1) * D], ones[:], bias_row[:], start=False, stop=True)
        return last

    def lane_buffers(stack, tag, names):
        b = {n: stack.enter_context(nc.sbuf_tensor(f"{n}_{tag}", [P, CH], F32)) for n in names.split()}
        for n, width in (("st", 6 * SUB), ("mv", 2 * SUB), ("sd", SUB), ("rs", SUB), ("nm", SUB)):
            b[n] = stack.enter_context(nc.sbuf_tensor(f"{n}_{tag}", [P, width], F32))
        return b

    def node_rows(table, it, L):
        return table[bass.ds((it * NL + L) * CH, CH), :].rearrange("(p j) f -> p (j f)", j=SUB)

    def node_loop(first, last, map_step):
        new_phase()
        with ExitStack() as tmp:
            B = [lane_buffers(tmp, f"n{first}_{L}", "x u v w x1 x1T h1T xw0 xw1 xw2 x2 x3 x4") for L in range(NL)]
            m_idx = tmp.enter_context(nc.sbuf_tensor(f"m_idx{first}", [P, max(MAP_W, 2 * MAP_R)], U32))
            m_val = tmp.enter_context(nc.sbuf_tensor(f"m_val{first}", [P, max(MAP_W, 2 * MAP_R)], U32))
            A = [ps[:, 2 * L, :] for L in range(NL)]
            C = [ps[:, 2 * L + 1, :] for L in range(NL)]
            lanes = range(NL)
            with nc.Fori(first, last) as it:
                with nc.Block() as block:
                    @block.sync
                    def _(sp):
                        for L in lanes:
                            sp.dma_start(B[L]["x"][:], node_rows(x, it, L)).then_inc(S(f"x_in{L}"), 16)
                        for k, (name, ready) in enumerate((("xw0", "xw0"), ("xw1", "xw1"), ("xw2", "xw2"),
                                                           ("x2", "c_out"), ("x3", "e_out"))):
                            for L in lanes:
                                sp.wait_ge(S(ready), L + 1)
                                sp.dma_start(node_rows(tables[k], it, L), B[L][name][:]).then_inc(S("stored"), 16)
                        for L in lanes:
                            sp.wait_ge(S("f_out"), L + 1)
                            sp.dma_start(node_rows(out, it, L), B[L]["x4"][:]).then_inc(S("stored"), 16)
                        sp.wait_ge(S("stored"), 16 * 6 * NL)

                    @block.gpsimd
                    def _(pool):
                        map_step(pool, it, m_idx, m_val)
                        for L in lanes:
                            b = B[L]
                            pool.wait_ge(S(f"x_in{L}"), 16)
                            nc.gpsimd.tensor_tensor(rows4(b["w"][:]), rows4(b["x"][:]), each_row(beta0), ALU.add).then_inc(S("xb"), 1)
                        for L in lanes:
                            b = B[L]
                            pool.wait_ge(S("xb"), L + 1)
                            nc.gpsimd.tensor_tensor(b["w"][:], b["w"][:], b["x"][:], ALU.add).then_inc(S("xxb"), 1)
                        for L in lanes:
                            b = B[L]
                            pool.wait_ge(S("c_out"), L + 1)
                            nc.gpsimd.tensor_tensor(rows4(b["w"][:]), rows4(b["x2"][:]), each_row(beta2), ALU.add).then_inc(S("x2b"), 1)

                    @block.tensor
                    def _(pe):
                        for L in lanes:
                            pe.wait_ge(S(f"x_in{L}"), 16)
                            turn(pe, A[L], B[L]["x"]).then_inc(S("xT_ps"), 1)
                        for L in lanes:
                            pe.wait_ge(S("xT"), L + 1)
                            rows_times(pe, C[L], B[L]["x1T"], W0).then_inc(S("h_ps"), 1)
                        for L in lanes:
                            pe.wait_ge(S("b_out"), L + 1)
                            turn(pe, A[L], B[L]["x1"]).then_inc(S("x1T_ps"), 1)
                        for L in lanes:
                            pe.wait_ge(S("x1T"), L + 1)
                            rows_times(pe, C[L], B[L]["x1T"], WI0, xw0_bias_row).then_inc(S("xw0_ps"), 1)
                            nc.tensor.matmul(A[L], WI0[:], B[L]["x1T"][:], start=True, stop=True).then_inc(S("h1_ps"), 1)
                        for L in lanes:
                            pe.wait_ge(S("h1T"), L + 1)
                            pe.wait_ge(S("xw0"), L + 1)
                            rows_times(pe, C[L], B[L]["h1T"], WS[1]).then_inc(S("xw1_ps"), 1)
                            nc.tensor.matmul(A[L], WS[1][:], B[L]["h1T"][:], start=True, stop=True).then_inc(S("h2_ps"), 1)
                        for L in lanes:
                            pe.wait_ge(S("h2T"), L + 1)
                            pe.wait_ge(S("xw1"), L + 1)
                            rows_times(pe, C[L], B[L]["x1T"], WS[2]).then_inc(S("xw2_ps"), 1)

                    @block.scalar
                    def _(act):
                        for L in lanes:
                            act.wait_ge(S("xT_ps"), L + 1)
                            nc.scalar.copy(B[L]["x1T"][:], A[L]).then_inc(S("xT"), 1)
                        for L in lanes:
                            b = B[L]
                            act.wait_ge(S("hb"), L + 1)
                            nc.scalar.activation(b["v"][:], b["u"][:], ACT.Gelu).then_inc(S("gelu"), 1)
                        for L in lanes:
                            ln_root(act, "a", L, B[L])
                        for L in lanes:
                            ln_apply(act, "a", L, B[L], B[L]["u"], B[L]["v"])
                        for L in lanes:
                            ln_root(act, "b", L, B[L])
                        for L in lanes:
                            ln_apply(act, "b", L, B[L], B[L]["x1"], B[L]["v"])
                        for L in lanes:
                            act.wait_ge(S("x1T_ps"), L + 1)
                            nc.scalar.copy(B[L]["x1T"][:], A[L]).then_inc(S("x1T"), 1)
                        for L in lanes:
                            act.wait_ge(S("xw0_ps"), L + 1)
                            nc.scalar.copy(B[L]["xw0"][:], C[L]).then_inc(S("xw0"), 1)
                            act.wait_ge(S("h1_ps"), L + 1)
                            nc.scalar.activation(B[L]["h1T"][:], A[L], ACT.Relu, bias=h1_bias[:, 0:1]).then_inc(S("h1T"), 1)
                        for L in lanes:
                            act.wait_ge(S("xw1_ps"), L + 1)
                            nc.scalar.copy(B[L]["xw1"][:], C[L]).then_inc(S("xw1"), 1)
                            act.wait_ge(S("h2_ps"), L + 1)
                            nc.scalar.activation(B[L]["x1T"][:], A[L], ACT.Relu, bias=h2_bias[:, 0:1]).then_inc(S("h2T"), 1)
                        for L in lanes:
                            act.wait_ge(S("xw2_ps"), L + 1)
                            nc.scalar.copy(B[L]["xw2"][:], C[L]).then_inc(S("xw2"), 1)
                        for L in lanes:
                            ln_root(act, "c", L, B[L])
                        for L in lanes:
                            ln_apply(act, "c", L, B[L], B[L]["x2"], B[L]["v"])
                        for L in lanes:
                            ln_root(act, "d", L, B[L])
                        for L in lanes:
                            ln_apply(act, "d", L, B[L], B[L]["v"], B[L]["u"])
                        for L in lanes:
                            ln_root(act, "e", L, B[L])
                        for L in lanes:
                            ln_apply(act, "e", L, B[L], B[L]["x3"], B[L]["u"])
                        for L in lanes:
                            ln_root(act, "f", L, B[L])
                        for L in lanes:
                            ln_apply(act, "f", L, B[L], B[L]["x4"], B[L]["v"])

                    @block.vector
                    def _(v):
                        V = nc.vector
                        for L in lanes:
                            v.wait_ge(S("h_ps"), L + 1)
                            V.tensor_tensor(rows4(B[L]["u"][:]), rows4(C[L]), each_row(bias0), ALU.add).then_inc(S("hb"), 1)
                        for L in lanes:
                            ln_stats(v, "a", L, B[L], B[L]["v"], "gelu")
                        for L in lanes:
                            ln_scale(v, "a", L, B[L])
                        for L in lanes:
                            b = B[L]
                            v.wait_ge(S("a_out"), L + 1)
                            V.tensor_tensor(rows4(b["u"][:]), rows4(b["u"][:]), each_row(gamma0), ALU.mult).then_inc(S("ag"), 1)
                        for L in lanes:
                            b = B[L]
                            v.wait_ge(S("ag"), L + 1)
                            v.wait_ge(S("xxb"), L + 1)
                            V.tensor_tensor(b["v"][:], b["u"][:], b["w"][:], ALU.add).then_inc(S("x1_pre"), 1)
                        for L in lanes:
                            ln_stats(v, "b", L, B[L], B[L]["v"], "x1_pre")
                        for L in lanes:
                            ln_scale(v, "b", L, B[L])
                        for L in lanes:
                            b = B[L]
                            v.wait_ge(S("xw2"), L + 1)
                            V.tensor_tensor(rows4(b["u"][:]), rows4(b["xw2"][:]), each_row(bs_row[2]), ALU.add).then_inc(S("h3_pre"), 1)
                        for L in lanes:
                            b = B[L]
                            v.wait_ge(S("h3_pre"), L + 1)
                            V.scalar_tensor_tensor(out=b["v"][:], in0=b["u"][:], scalar=0.0, in1=b["x1"][:],
                                                   op0=ALU.max, op1=ALU.add).then_inc(S("x2_pre"), 1)
                        for L in lanes:
                            ln_stats(v, "c", L, B[L], B[L]["v"], "x2_pre")
                        for L in lanes:
                            ln_scale(v, "c", L, B[L])
                        for L in lanes:
                            b = B[L]
                            v.wait_ge(S("c_out"), L + 1)
                            V.tensor_tensor(rows4(b["u"][:]), rows4(b["x2"][:]), each_row(bo), ALU.add).then_inc(S("h_res"), 1)
                        for L in lanes:
                            ln_stats(v, "d", L, B[L], B[L]["u"], "h_res")
                        for L in lanes:
                            ln_scale(v, "d", L, B[L])
                        for L in lanes:
                            b = B[L]
                            v.wait_ge(S("d_out"), L + 1)
                            V.tensor_tensor(rows4(b["v"][:]), rows4(b["v"][:]), each_row(gamma2), ALU.mult).then_inc(S("dg"), 1)
                        for L in lanes:
                            b = B[L]
                            v.wait_ge(S("dg"), L + 1)
                            v.wait_ge(S("x2b"), L + 1)
                            V.tensor_tensor(b["u"][:], b["v"][:], b["w"][:], ALU.add).then_inc(S("x3_pre"), 1)
                        for L in lanes:
                            ln_stats(v, "e", L, B[L], B[L]["u"], "x3_pre")
                        for L in lanes:
                            ln_scale(v, "e", L, B[L])
                        for L in lanes:
                            b = B[L]
                            v.wait_ge(S("e_out"), L + 1)
                            V.tensor_tensor(rows4(b["v"][:]), rows4(b["x3"][:]), each_row(bias3), ALU.add).then_inc(S("x4_pre"), 1)
                        for L in lanes:
                            ln_stats(v, "f", L, B[L], B[L]["v"], "x4_pre")
                        for L in lanes:
                            ln_scale(v, "f", L, B[L])
                all_meet()

    def write_map(pool, it, m_idx, m_val):
        nc.gpsimd.tensor_copy(m_idx[:, 0:MAP_W], end_idx[:, bass.ds(it * MAP_W, MAP_W)]).then_inc(S("m_idx"), 1)
        nc.gpsimd.tensor_copy(m_val[:, 0:MAP_W], slot_no[:, bass.ds(it * MAP_W, MAP_W)]).then_inc(S("m_idx"), 1)
        pool.wait_ge(S("m_idx"), 2)
        for t in range(MAP_W):
            pool.indirect_dma_start(out=node_map, out_offset=bass.IndirectOffsetOnAxis(ap=m_idx[:, t:t + 1], axis=0),
                                    in_=m_val[:, t:t + 1], in_offset=None,
                                    bounds_check=NT - 1, oob_is_err=False).then_inc(pool_dma["map_written"], 16)
        pool.wait_ge(pool_dma["map_written"], (it + 1) * (16 * MAP_W))

    def read_map(pool, it, m_idx, m_val):
        at = (it - MAP_IT) * MAP_R
        for k, of in enumerate((src_idx, dst_idx)):
            nc.gpsimd.tensor_copy(m_idx[:, k * MAP_R:(k + 1) * MAP_R], of[:, bass.ds(at, MAP_R)]).then_inc(S("m_idx"), 1)
        pool.wait_ge(S("m_idx"), 2)
        for t in range(2 * MAP_R):
            pool.indirect_dma_start(out=m_val[:, t:t + 1], out_offset=None, in_=node_map,
                                    in_offset=bass.IndirectOffsetOnAxis(ap=m_idx[:, t:t + 1], axis=0),
                                    bounds_check=NT - 1, oob_is_err=False).then_inc(pool_dma["map_read"], 16)
        pool.wait_ge(pool_dma["map_read"], (it - (MAP_IT - 1)) * (16 * 2 * MAP_R))
        for k, to in enumerate((slot_idx, own_idx)):
            nc.gpsimd.tensor_copy(to[:, bass.ds(at, MAP_R)], m_val[:, k * MAP_R:(k + 1) * MAP_R])

    node_loop(0, MAP_IT, write_map)
    node_loop(MAP_IT, N_IT, read_map)

    def slot_rows(table, it, L, base=NT):
        return table[bass.ds(base + (it * EL + L) * CH, CH), :].rearrange("(j p) f -> p j f", p=P)

    def edge_cols(row, it, L, parts=P):
        return row[:, bass.ds((it * EL + L) * CH, CH)].to_broadcast([parts, CH])

    lanes = range(EL)

    def gather(pool, table, rows, idx, to, signal):
        for t in range(SUB):
            pool.indirect_dma_start(out=to[:, t * D:(t + 1) * D], out_offset=None, in_=table,
                                    in_offset=bass.IndirectOffsetOnAxis(ap=idx[:, t:t + 1], axis=0),
                                    bounds_check=rows - 1, oob_is_err=False).then_inc(signal, 16)

    class Hop:

        def __init__(self, stack, tag, names, gathers):
            self.B = [lane_buffers(stack, f"{tag}_{L}", names) for L in lanes]
            for L in lanes:
                self.B[L]["M"] = stack.enter_context(nc.sbuf_tensor(f"M_{tag}_{L}", [P, CH + 1], F32))
            self.idx = {g: stack.enter_context(nc.sbuf_tensor(f"idx_{tag}_{g}", [P, IT_TILES], U32)) for g in gathers}
            self.dis = stack.enter_context(nc.sbuf_tensor(f"dis_{tag}", [P, IT_TILES], F32))
            self.gathers = gathers
            self.gathered = pool_dma[f"gathered_{tag}"]
            self.per_it = 16 * IT_TILES * len(gathers)

        def start(self, init):
            new_phase()
            with nc.Block() as block:
                @block.gpsimd
                def _(pool):
                    for g, (table, rows, idx) in self.gathers.items():
                        nc.gpsimd.tensor_copy(self.idx[g][:], idx[:, 0:IT_TILES]).then_inc(S("idx"), 1)
                    pool.wait_ge(S("idx"), len(self.gathers))
                    for g, (table, rows, idx) in self.gathers.items():
                        for L in lanes:
                            gather(pool, table, rows, self.idx[g][:, L * SUB:(L + 1) * SUB], self.B[L][g], self.gathered)
                    pool.wait_ge(self.gathered, self.per_it)

                @block.vector
                def _(v):
                    for L in lanes:
                        for n, value in init.items():
                            nc.vector.memset(self.B[L][n][:], value)
            all_meet()

        def gather_next(self, pool, it, free):
            for g, (table, rows, idx) in self.gathers.items():
                nc.gpsimd.tensor_copy(self.idx[g][:], idx[:, bass.ds((it + 1) * IT_TILES, IT_TILES)]).then_inc(S("idx"), 1)
            pool.wait_ge(S("idx"), len(self.gathers))
            for L in lanes:
                for g, (table, rows, idx) in self.gathers.items():
                    for name in free[g]:
                        pool.wait_ge(S(name), L + 1)
                    gather(pool, table, rows, self.idx[g][:, L * SUB:(L + 1) * SUB], self.B[L][g], self.gathered)
            pool.wait_ge(self.gathered, (it + 2) * self.per_it)

    def run_maximum(v, B, L, score, ready):
        V = nc.vector
        b, before = B[L], B[(L - 1) % EL]
        for name in ready:
            v.wait_ge(S(name), L + 1)
        v.wait_ge(S(f"pen_in{L}"), 16)
        if L:
            v.wait_ge(S("M"), L)
        V.tensor_copy(b["M"][:, 0:1], before["M"][:, CH:CH + 1]).then_inc(S("M_first"), 1)
        v.wait_ge(S("M_first"), L + 1)
        V.tensor_tensor_scan(b["M"][:, 1:CH + 1], b["pen"][:], score, b["M"][:, 0:1], ALU.min, ALU.max).then_inc(S("M"), 1)
        V.tensor_tensor(b["Dm"][:, 0:1], b["pen"][:, 0:1], b["M"][:, 0:1], ALU.min).then_inc(S("Dm0"), 1)
        v.wait_ge(S("M"), L + 1)
        V.tensor_tensor(b["Dm"][:, 1:CH], b["pen"][:, 1:CH], b["M"][:, 1:CH], ALU.min).then_inc(S("Dm0"), 1)
        V.tensor_tensor(b["dz"][:], score, b["M"][:, 1:CH + 1], ALU.subtract).then_inc(S("dz"), 1)
        v.wait_ge(S("Dm0"), 2 * (L + 1))
        V.tensor_tensor(b["Dm"][:], b["Dm"][:], b["M"][:, 1:CH + 1], ALU.subtract).then_inc(S("Dm"), 1)

    def run_weights(act, B, L):
        b = B[L]
        act.wait_ge(S("dz"), L + 1)
        nc.scalar.activation(b["p"][:], b["dz"][:], ACT.Exp).then_inc(S("p"), 1)
        act.wait_ge(S("Dm"), L + 1)
        nc.scalar.activation(b["F"][:], b["Dm"][:], ACT.Exp).then_inc(S("F"), 1)

    def run_sums(v, B, L, value, bias, ready):
        V = nc.vector
        b, before = B[L], B[(L - 1) % EL]
        v.wait_ge(S("p"), L + 1)
        v.wait_ge(S(ready), L + 1)
        V.scalar_tensor_tensor(out=b["msg"][:], in0=value, scalar=bias, in1=b["p"][:],
                               op0=ALU.add, op1=ALU.mult).then_inc(S("msg"), 1)
        v.wait_ge(S("F"), L + 1)
        if L:
            v.wait_ge(S("den"), L)
            v.wait_ge(S("num"), L)
        V.tensor_tensor_scan(b["den"][:], b["F"][:], b["p"][:], before["den"][:, CH - 1:CH], ALU.mult, ALU.add).then_inc(S("den"), 1)
        v.wait_ge(S("msg"), L + 1)
        V.tensor_tensor_scan(b["num"][:], b["F"][:], b["msg"][:], before["num"][:, CH - 1:CH], ALU.mult, ALU.add).then_inc(S("num"), 1)

    def den_rows(pe, to, den, sel, heads):
        for j in range(SUB):
            last = nc.tensor.matmul(to[:, j * heads:(j + 1) * heads], den[:, j * P:(j + 1) * P], sel[:], start=True, stop=True)
        return last

    def divide(v, b, L, num_rows, den_r, heads, eps_den, to, ready):
        V = nc.vector
        n = SUB * heads
        v.wait_ge(S(ready), L + 1)
        V.tensor_scalar(b["dn"][:, 0:n], den_r[:, 0:n], eps_den, None, ALU.add).then_inc(S("dn"), 1)
        v.wait_ge(S("dn"), L + 1)
        V.reciprocal(b["rd"][:, 0:n], b["dn"][:, 0:n]).then_inc(S("rd"), 1)
        v.wait_ge(S("rd"), L + 1)
        c = D // heads
        V.tensor_tensor(to.rearrange("p (n c) -> p n c", c=c), num_rows.rearrange("p (n c) -> p n c", c=c),
                        by_row(b["rd"][:, 0:n], c), ALU.mult).then_inc(S("divided"), 1)

    Q = [[ps[:, 4 * L + k, :] for k in range(4)] for L in lanes]

    with ExitStack() as tmp:
        hop = Hop(tmp, "h0", "gs gd xd xsT xdT pen z zs Dm dz dzs p pself F den num msg u v w x1 x1T xw dn rd",
                  {"gs": (x, NT, src_idx), "gd": (x, NT, dst_idx)})
        B = hop.B
        hop.start({"M": 0.0, "den": 0.0, "num": 0.0})
        with nc.Fori(0, E_IT) as it:
            with nc.Block() as block:
                @block.sync
                def _(sp):
                    for L in lanes:
                        sp.dma_start(B[L]["pen"][:], edge_cols(pen_row, it, L)).then_inc(S(f"pen_in{L}"), 16)
                    for L in lanes:
                        sp.wait_ge(S("b_out"), L + 1)
                        sp.dma_start(slot_rows(x1_slots, it, L, 0), rows4(B[L]["x1"][:])).then_inc(S("stored"), 16)
                    for L in lanes:
                        sp.wait_ge(S("xw"), L + 1)
                        sp.dma_start(slot_rows(tables[0], it, L), rows4(B[L]["xw"][:])).then_inc(S("stored"), 16)
                    sp.wait_ge(S("stored"), 16 * 2 * EL)

                @block.gpsimd
                def _(pool):
                    for L in lanes:
                        nc.gpsimd.tensor_copy(B[L]["xd"][:], B[L]["gd"][:]).then_inc(S("xd"), 1)
                    hop.gather_next(pool, it, {"gs": ["xsT_ps"], "gd": ["xdT_ps", "xd"]})
                    for L in lanes:
                        b = B[L]
                        pool.wait_ge(S("xd"), L + 1)
                        nc.gpsimd.tensor_tensor(rows4(b["w"][:]), rows4(b["xd"][:]), each_row(beta0), ALU.add).then_inc(S("xb"), 1)
                    for L in lanes:
                        b = B[L]
                        pool.wait_ge(S("xb"), L + 1)
                        nc.gpsimd.tensor_tensor(b["w"][:], b["w"][:], b["xd"][:], ALU.add).then_inc(S("xxb"), 1)

                @block.tensor
                def _(pe):
                    for L in lanes:
                        turn(pe, Q[L][0], B[L]["gs"]).then_inc(S("xsT_ps"), 1)
                        turn(pe, Q[L][1], B[L]["gd"]).then_inc(S("xdT_ps"), 1)
                    for L in lanes:
                        b = B[L]
                        pe.wait_ge(S("xsT"), L + 1)
                        pe.wait_ge(S("xdT"), L + 1)
                        nc.tensor.matmul(Q[L][1], src_rep[:], b["xsT"][:], start=True, stop=False)
                        nc.tensor.matmul(Q[L][1], dst_rep[:], b["xdT"][:], start=False, stop=True).then_inc(S("z_ps"), 1)
                        nc.tensor.matmul(Q[L][2], self_rep[:], b["xdT"][:], start=True, stop=True).then_inc(S("zs_ps"), 1)
                        nc.tensor.matmul(Q[L][0], W0[:], b["xsT"][:], start=True, stop=True).then_inc(S("hs_ps"), 1)
                        nc.tensor.matmul(Q[L][3], W0[:], b["xdT"][:], start=True, stop=True).then_inc(S("hd_ps"), 1)
                    for L in lanes:
                        b = B[L]
                        pe.wait_ge(S("num_self"), L + 1)
                        pe.wait_ge(S("den_self"), L + 1)
                        turn_back = [nc.tensor.transpose(Q[L][1][:, j * P:(j + 1) * P], b["u"][:, j * P:(j + 1) * P], ident[:]) for j in range(SUB)]
                        den_rows(pe, Q[L][2], b["v"], sel4, 4).then_inc(S("num_rows"), 1)
                    for L in lanes:
                        pe.wait_ge(S("b_out"), L + 1)
                        turn(pe, Q[L][0], B[L]["x1"]).then_inc(S("x1T_ps"), 1)
                    for L in lanes:
                        pe.wait_ge(S("x1T"), L + 1)
                        rows_times(pe, Q[L][1], B[L]["x1T"], WI0, xw0_bias_row).then_inc(S("xw_ps"), 1)

                @block.scalar
                def _(act):
                    for L in lanes:
                        act.wait_ge(S("xsT_ps"), L + 1)
                        nc.scalar.copy(B[L]["xsT"][:], Q[L][0]).then_inc(S("xsT"), 1)
                        act.wait_ge(S("xdT_ps"), L + 1)
                        nc.scalar.copy(B[L]["xdT"][:], Q[L][1]).then_inc(S("xdT"), 1)
                    for L in lanes:
                        b = B[L]
                        act.wait_ge(S("z_ps"), L + 1)
                        nc.scalar.copy(b["z"][:], Q[L][1]).then_inc(S("z"), 1)
                        act.wait_ge(S("zs_ps"), L + 1)
                        nc.scalar.copy(b["zs"][:], Q[L][2]).then_inc(S("zs"), 1)
                    for L in lanes:
                        b = B[L]
                        run_weights(act, B, L)
                        act.wait_ge(S("dzs"), L + 1)
                        nc.scalar.activation(b["pself"][:], b["dzs"][:], ACT.Exp).then_inc(S("pself"), 1)
                    for L in lanes:
                        b = B[L]
                        act.wait_ge(S("ob"), L + 1)
                        nc.scalar.activation(b["v"][:], b["msg"][:], ACT.Gelu).then_inc(S("gelu"), 1)
                    for L in lanes:
                        ln_root(act, "a", L, B[L])
                    for L in lanes:
                        ln_apply(act, "a", L, B[L], B[L]["u"], B[L]["v"])
                    for L in lanes:
                        ln_root(act, "b", L, B[L])
                    for L in lanes:
                        ln_apply(act, "b", L, B[L], B[L]["x1"], B[L]["v"])
                    for L in lanes:
                        act.wait_ge(S("x1T_ps"), L + 1)
                        nc.scalar.copy(B[L]["x1T"][:], Q[L][0]).then_inc(S("x1T"), 1)

                @block.vector
                def _(v):
                    V = nc.vector
                    V.tensor_copy(hop.dis[:], dis[:, bass.ds(it * IT_TILES, IT_TILES)]).then_inc(S("dis"), 1)
                    for L in lanes:
                        b = B[L]
                        v.wait_ge(S("z"), L + 1)
                        V.scalar_tensor_tensor(out=b["z"][:], in0=b["z"][:], scalar=0.2, in1=b["z"][:], op0=ALU.mult, op1=ALU.max).then_inc(S("zl"), 1)
                        v.wait_ge(S("zs"), L + 1)
                        V.scalar_tensor_tensor(out=b["zs"][:], in0=b["zs"][:], scalar=0.2, in1=b["zs"][:], op0=ALU.mult, op1=ALU.max).then_inc(S("zsl"), 1)
                    for L in lanes:
                        b = B[L]
                        v.wait_ge(S("zl"), L + 1)
                        v.wait_ge(S("zsl"), L + 1)
                        V.tensor_tensor(b["u"][:], b["z"][:], b["zs"][:], ALU.max).then_inc(S("zm"), 1)
                    for L in lanes:
                        b, before = B[L], B[(L - 1) % EL]
                        v.wait_ge(S("zm"), L + 1)
                        v.wait_ge(S(f"pen_in{L}"), 16)
                        if L:
                            v.wait_ge(S("M"), L)
                        V.tensor_copy(b["M"][:, 0:1], before["M"][:, CH:CH + 1]).then_inc(S("M_first"), 1)
                        v.wait_ge(S("M_first"), L + 1)
                        V.tensor_tensor_scan(b["M"][:, 1:CH + 1], b["pen"][:], b["u"][:], b["M"][:, 0:1], ALU.min, ALU.max).then_inc(S("M"), 1)
                    for L in lanes:
                        b = B[L]
                        v.wait_ge(S("M"), L + 1)
                        V.tensor_tensor(b["Dm"][:], b["pen"][:], b["M"][:, 0:CH], ALU.min).then_inc(S("Dm0"), 1)
                        V.tensor_tensor(b["dz"][:], b["z"][:], b["M"][:, 1:CH + 1], ALU.subtract).then_inc(S("dz"), 1)
                        V.tensor_tensor(b["dzs"][:], b["zs"][:], b["M"][:, 1:CH + 1], ALU.subtract).then_inc(S("dzs"), 1)
                        v.wait_ge(S("Dm0"), L + 1)
                        V.tensor_tensor(b["Dm"][:], b["Dm"][:], b["M"][:, 1:CH + 1], ALU.subtract).then_inc(S("Dm"), 1)
                    for L in lanes:
                        run_sums(v, B, L, Q[L][0], 0.0, "hs_ps")
                    for L in lanes:
                        b = B[L]
                        v.wait_ge(S("pself"), L + 1)
                        v.wait_ge(S("hd_ps"), L + 1)
                        V.tensor_tensor(b["msg"][:], b["pself"][:], Q[L][3], ALU.mult).then_inc(S("self_msg"), 1)
                        v.wait_ge(S("den"), L + 1)
                        V.tensor_tensor(b["v"][:], b["den"][:], b["pself"][:], ALU.add).then_inc(S("den_self"), 1)
                        v.wait_ge(S("self_msg"), L + 1)
                        v.wait_ge(S("num"), L + 1)
                        V.tensor_tensor(b["u"][:], b["num"][:], b["msg"][:], ALU.add).then_inc(S("num_self"), 1)
                    for L in lanes:
                        divide(v, B[L], L, Q[L][1], Q[L][2], 4, 1e-16, B[L]["dz"], "num_rows")
                    for L in lanes:
                        b = B[L]
                        v.wait_ge(S("divided"), L + 1)
                        V.tensor_tensor(rows4(b["msg"][:]), rows4(b["dz"][:]), each_row(bias0), ALU.add).then_inc(S("ob"), 1)
                    for L in lanes:
                        ln_stats(v, "a", L, B[L], B[L]["v"], "gelu")
                    for L in lanes:
                        ln_scale(v, "a", L, B[L])
                    for L in lanes:
                        b = B[L]
                        v.wait_ge(S("a_out"), L + 1)
                        V.tensor_tensor(rows4(b["u"][:]), rows4(b["u"][:]), each_row(gamma0), ALU.mult).then_inc(S("ag"), 1)
                    for L in lanes:
                        b = B[L]
                        v.wait_ge(S("ag"), L + 1)
                        v.wait_ge(S("xxb"), L + 1)
                        V.tensor_tensor(b["v"][:], b["u"][:], b["w"][:], ALU.add).then_inc(S("x1_pre"), 1)
                    for L in lanes:
                        ln_stats(v, "b", L, B[L], B[L]["v"], "x1_pre")
                    for L in lanes:
                        ln_scale(v, "b", L, B[L])
                    for L in lanes:
                        b = B[L]
                        v.wait_ge(S("xw_ps"), L + 1)
                        v.wait_ge(S("dis"), 1)
                        V.tensor_tensor(rows4(b["xw"][:]), rows4(Q[L][1]), by_row(hop.dis[:, L * SUB:(L + 1) * SUB]), ALU.mult).then_inc(S("xw"), 1)
            all_meet()

    for layer in range(3):
        last_layer = layer == 2
        with ExitStack() as tmp:
            hop = Hop(tmp, f"g{layer}", "gs own nst agg u v w hT xw x1 x2", {"gs": (tables[layer], NT + ET, slot_idx)})
            B = hop.B
            hop.start({"agg": 0.0})
            with nc.Fori(0, E_IT) as it:
                with nc.Block() as block:
                    @block.sync
                    def _(sp):
                        for L in lanes:
                            sp.dma_start(B[L]["nst"][:], edge_cols(nst_row, it, L)).then_inc(S(f"nst_in{L}"), 16)
                        for L in lanes:
                            sp.dma_start(rows4(B[L]["own"][:]), slot_rows(tables[layer], it, L)).then_inc(S(f"own_in{L}"), 16)
                        if last_layer:
                            for L in lanes:
                                sp.dma_start(rows4(B[L]["x1"][:]), slot_rows(x1_slots, it, L, 0)).then_inc(S(f"x1_in{L}"), 16)
                        for L in lanes:
                            sp.wait_ge(S("c_out" if last_layer else "xw"), L + 1)
                            new = B[L]["x2" if last_layer else "xw"]
                            sp.dma_start(slot_rows(tables[layer + 1], it, L), rows4(new[:])).then_inc(S("stored"), 16)
                        sp.wait_ge(S("stored"), 16 * EL)

                    @block.gpsimd
                    def _(pool):
                        hop.gather_next(pool, it, {"gs": ["xsT_ps"]})

                    @block.tensor
                    def _(pe):
                        for L in lanes:
                            turn(pe, Q[L][0], B[L]["gs"]).then_inc(S("xsT_ps"), 1)
                        for L in lanes:
                            pe.wait_ge(S("agg"), L + 1)
                            turn(pe, Q[L][1], B[L]["agg"]).then_inc(S("agg_rows"), 1)
                        if not last_layer:
                            for L in lanes:
                                pe.wait_ge(S("h_pre"), L + 1)
                                turn(pe, Q[L][2], B[L]["v"]).then_inc(S("hT_ps"), 1)
                            for L in lanes:
                                pe.wait_ge(S("hT"), L + 1)
                                rows_times(pe, Q[L][3], B[L]["hT"], WS[layer + 1]).then_inc(S("xw_ps"), 1)

                    @block.scalar
                    def _(act):
                        if not last_layer:
                            for L in lanes:
                                act.wait_ge(S("hT_ps"), L + 1)
                                nc.scalar.activation(B[L]["hT"][:], Q[L][2], ACT.Relu).then_inc(S("hT"), 1)
                        else:
                            for L in lanes:
                                ln_root(act, "c", L, B[L])
                            for L in lanes:
                                ln_apply(act, "c", L, B[L], B[L]["x2"], B[L]["u"])

                    @block.vector
                    def _(v):
                        V = nc.vector
                        V.tensor_copy(hop.dis[:], dis[:, bass.ds(it * IT_TILES, IT_TILES)]).then_inc(S("dis"), 1)
                        for L in lanes:
                            b, before = B[L], B[(L - 1) % EL]
                            v.wait_ge(S("xsT_ps"), L + 1)
                            v.wait_ge(S(f"nst_in{L}"), 16)
                            if L:
                                v.wait_ge(S("agg"), L)
                            V.tensor_tensor_scan(b["agg"][:], b["nst"][:], Q[L][0], before["agg"][:, CH - 1:CH], ALU.mult, ALU.add).then_inc(S("agg"), 1)
                        for L in lanes:
                            b = B[L]
                            v.wait_ge(S("agg_rows"), L + 1)
                            v.wait_ge(S(f"own_in{L}"), 16)
                            V.tensor_tensor(b["u"][:], Q[L][1], b["own"][:], ALU.add).then_inc(S("with_self"), 1)
                        for L in lanes:
                            b = B[L]
                            v.wait_ge(S("with_self"), L + 1)
                            v.wait_ge(S("dis"), 1)
                            V.tensor_tensor(rows4(b["w"][:]), rows4(b["u"][:]), by_row(hop.dis[:, L * SUB:(L + 1) * SUB]), ALU.mult).then_inc(S("scaled"), 1)
                        for L in lanes:
                            b = B[L]
                            v.wait_ge(S("scaled"), L + 1)
                            V.tensor_tensor(rows4(b["v"][:]), rows4(b["w"][:]), each_row(bs_row[layer]), ALU.add).then_inc(S("h_pre"), 1)
                        if not last_layer:
                            for L in lanes:
                                b = B[L]
                                v.wait_ge(S("xw_ps"), L + 1)
                                V.tensor_tensor(rows4(b["xw"][:]), rows4(Q[L][3]), by_row(hop.dis[:, L * SUB:(L + 1) * SUB]), ALU.mult).then_inc(S("xw"), 1)
                        else:
                            for L in lanes:
                                b = B[L]
                                v.wait_ge(S("h_pre"), L + 1)
                                v.wait_ge(S(f"x1_in{L}"), 16)
                                V.scalar_tensor_tensor(out=b["u"][:], in0=b["v"][:], scalar=0.0, in1=b["x1"][:],
                                                       op0=ALU.max, op1=ALU.add).then_inc(S("x2_pre"), 1)
                            for L in lanes:
                                ln_stats(v, "c", L, B[L], B[L]["u"], "x2_pre")
                            for L in lanes:
                                ln_scale(v, "c", L, B[L])
                all_meet()

    for kind in (2, 3):
        heads = 8 if kind == 2 else 4
        width = 32 if kind == 2 else 64
        table, ea = tables[kind + 1], (ea32 if kind == 2 else ea64)
        with ExitStack() as tmp:
            hop = Hop(tmp, f"t{kind}", "gs own xsT xdT pen kb qk z Dm dz p F den num msg o oT u v w xo xn dn rd",
                      {"gs": (table, NT + ET, slot_idx), "own": (table, NT + ET, own_idx)})
            B = hop.B
            for L in lanes:
                B[L]["ea"] = tmp.enter_context(nc.sbuf_tensor(f"ea_{kind}_{L}", [P, SUB * width], F32))
                B[L]["eaT"] = tmp.enter_context(nc.sbuf_tensor(f"eaT_{kind}_{L}", [width + 1, CH], F32))
            end_now = tmp.enter_context(nc.sbuf_tensor(f"end_now{kind}", [P, IT_TILES], U32))
            hop.start({"M": 0.0, "den": 0.0, "num": 0.0, "eaT": 1.0})
            with nc.Fori(0, E_IT) as it:
                with nc.Block() as block:
                    @block.sync
                    def _(sp):
                        for L in lanes:
                            b = B[L]
                            sp.dma_start(b["ea"].rearrange("p (j f) -> p j f", j=SUB), slot_rows(ea, it, L, 0)).then_inc(S(f"ea_in{L}"), 16)
                            sp.dma_start(b["pen"][:], edge_cols(pen_row, it, L)).then_inc(S(f"pen_in{L}"), 16)
                            if kind == 3:
                                sp.dma_start(b["eaT"][64:65, :], edge_cols(ew, it, L, 1)).then_inc(S(f"ew_in{L}"), 16)
                        if kind == 2:
                            for L in lanes:
                                sp.wait_ge(S("e_out"), L + 1)
                                sp.dma_start(slot_rows(tables[4], it, L), rows4(B[L]["xn"][:])).then_inc(S("stored"), 16)
                            sp.wait_ge(S("stored"), 16 * EL)

                    @block.gpsimd
                    def _(pool):
                        for L in lanes:
                            b = B[L]
                            nc.gpsimd.tensor_tensor(rows4(b["xo"][:]), rows4(b["own"][:]), each_row(bo if kind == 2 else bias3), ALU.add).then_inc(S("xo"), 1)
                            if kind == 2:
                                nc.gpsimd.tensor_tensor(rows4(b["w"][:]), rows4(b["own"][:]), each_row(beta2), ALU.add).then_inc(S("x2b"), 1)
                        hop.gather_next(pool, it, {"gs": ["xsT_ps"], "own": ["xdT_ps", "xo"] + ["x2b"] * (kind == 2)})
                        if kind == 3:
                            nc.gpsimd.tensor_copy(end_now[:], end_idx[:, bass.ds(it * IT_TILES, IT_TILES)]).then_inc(S("end_now"), 1)
                            pool.wait_ge(S("end_now"), 1)
                            for L in lanes:
                                pool.wait_ge(S("f_out"), L + 1)
                                for j in range(SUB):
                                    t = L * SUB + j
                                    pool.indirect_dma_start(out=out, out_offset=bass.IndirectOffsetOnAxis(ap=end_now[:, t:t + 1], axis=0),
                                                            in_=B[L]["xn"][:, j * D:(j + 1) * D], in_offset=None,
                                                            bounds_check=NODES - 1, oob_is_err=False).then_inc(pool_dma["scattered"], 16)
                            pool.wait_ge(pool_dma["scattered"], (it + 1) * (16 * IT_TILES))

                    @block.tensor
                    def _(pe):
                        for L in lanes:
                            b = B[L]
                            turn(pe, Q[L][0], b["gs"]).then_inc(S("xsT_ps"), 1)
                            turn(pe, Q[L][1], b["own"]).then_inc(S("xdT_ps"), 1)
                            pe.wait_ge(S(f"ea_in{L}"), 16)
                            turn(pe, Q[L][2], b["ea"], width).then_inc(S("eaT_ps"), 1)
                        for L in lanes:
                            b = B[L]
                            pe.wait_ge(S("xsT"), L + 1)
                            pe.wait_ge(S("xdT"), L + 1)
                            if kind == 2:
                                nc.tensor.matmul(Q[L][0], Wk[:], b["xsT"][:], start=True, stop=True).then_inc(S("k_ps"), 1)
                                nc.tensor.matmul(Q[L][1], Wq[:], b["xdT"][:], start=True, stop=True).then_inc(S("q_ps"), 1)
                                nc.tensor.matmul(Q[L][3], Wv[:], b["xsT"][:], start=True, stop=True).then_inc(S("v_ps"), 1)
                            else:
                                pe.wait_ge(S("eaT"), L + 1)
                                pe.wait_ge(S(f"ew_in{L}"), 16)
                                nc.tensor.matmul(Q[L][1], k3_rep[:], b["xsT"][:], start=True, stop=False)
                                nc.tensor.matmul(Q[L][1], q3_rep[:], b["xdT"][:], start=False, stop=False)
                                nc.tensor.matmul(Q[L][1], we3_rep[:], b["eaT"][:], start=False, stop=True).then_inc(S("z_ps"), 1)
                                nc.tensor.matmul(Q[L][3], Wv3[:], b["xsT"][:], start=True, stop=True).then_inc(S("v_ps"), 1)
                        if kind == 2:
                            for L in lanes:
                                b = B[L]
                                pe.wait_ge(S("eaT"), L + 1)
                                nc.tensor.matmul(Q[L][2], we2_rep[:], b["eaT"][:], start=True, stop=False)
                                pe.wait_ge(S("qk"), L + 1)
                                nc.tensor.matmul(Q[L][2], head_sum[:], b["qk"][:], start=False, stop=True).then_inc(S("z_ps"), 1)
                        for L in lanes:
                            b = B[L]
                            pe.wait_ge(S("num"), L + 1)
                            turn(pe, Q[L][0], b["num"])
                            den_rows(pe, Q[L][1], b["den"], sel8 if kind == 2 else sel4, heads).then_inc(S("num_rows"), 1)
                        if kind == 2:
                            for L in lanes:
                                pe.wait_ge(S("divided"), L + 1)
                                turn(pe, Q[L][2], B[L]["o"]).then_inc(S("oT_ps"), 1)
                            for L in lanes:
                                pe.wait_ge(S("oT"), L + 1)
                                rows_times(pe, Q[L][3], B[L]["oT"], Wo).then_inc(S("wo_ps"), 1)

                    @block.scalar
                    def _(act):
                        for L in lanes:
                            b = B[L]
                            act.wait_ge(S("xsT_ps"), L + 1)
                            nc.scalar.copy(b["xsT"][:], Q[L][0]).then_inc(S("xsT"), 1)
                            act.wait_ge(S("xdT_ps"), L + 1)
                            nc.scalar.copy(b["xdT"][:], Q[L][1]).then_inc(S("xdT"), 1)
                            act.wait_ge(S("eaT_ps"), L + 1)
                            nc.scalar.copy(b["eaT"][0:width, :], Q[L][2][0:width, :]).then_inc(S("eaT"), 1)
                        for L in lanes:
                            b = B[L]
                            if kind == 2:
                                act.wait_ge(S("k_ps"), L + 1)
                                nc.scalar.activation(b["kb"][:], Q[L][0], ACT.Identity, bias=bk[:, 0:1]).then_inc(S("kb"), 1)
                            else:
                                act.wait_ge(S("z_ps"), L + 1)
                                nc.scalar.mul(b["kb"][:], Q[L][1], float(32.0 ** -0.5)).then_inc(S("kb"), 1)
                        for L in lanes:
                            run_weights(act, B, L)
                        if kind == 2:
                            for L in lanes:
                                act.wait_ge(S("oT_ps"), L + 1)
                                nc.scalar.copy(B[L]["oT"][:], Q[L][2]).then_inc(S("oT"), 1)
                            for L in lanes:
                                ln_root(act, "d", L, B[L])
                            for L in lanes:
                                ln_apply(act, "d", L, B[L], B[L]["v"], B[L]["u"])
                            for L in lanes:
                                ln_root(act, "e", L, B[L])
                            for L in lanes:
                                ln_apply(act, "e", L, B[L], B[L]["xn"], B[L]["u"])
                        else:
                            for L in lanes:
                                ln_root(act, "f", L, B[L])
                            for L in lanes:
                                ln_apply(act, "f", L, B[L], B[L]["xn"], B[L]["u"])

                    @block.vector
                    def _(v):
                        V = nc.vector
                        for L in lanes:
                            b = B[L]
                            v.wait_ge(S("kb"), L + 1)
                            if kind == 2:
                                v.wait_ge(S("q_ps"), L + 1)
                                V.scalar_tensor_tensor(out=b["qk"][:], in0=Q[L][1], scalar=bq[:, 0:1], in1=b["kb"][:],
                                                       op0=ALU.add, op1=ALU.mult).then_inc(S("qk"), 1)
                            else:
                                V.scalar_tensor_tensor(out=b["z"][:], in0=b["kb"][:], scalar=0.2, in1=b["kb"][:],
                                                       op0=ALU.mult, op1=ALU.max).then_inc(S("zl"), 1)
                        for L in lanes:
                            run_maximum(v, B, L, Q[L][2] if kind == 2 else B[L]["z"][:], ["z_ps"] if kind == 2 else ["zl"])
                        for L in lanes:
                            run_sums(v, B, L, Q[L][3], bv[:, 0:1] if kind == 2 else 0.0, "v_ps")
                        for L in lanes:
                            divide(v, B[L], L, Q[L][0], Q[L][1], heads, 1e-8 if kind == 2 else 1e-16, B[L]["o"], "num_rows")
                        if kind == 2:
                            for L in lanes:
                                b = B[L]
                                v.wait_ge(S("wo_ps"), L + 1)
                                v.wait_ge(S("xo"), L + 1)
                                V.tensor_tensor(b["u"][:], Q[L][3], b["xo"][:], ALU.add).then_inc(S("h_res"), 1)
                            for L in lanes:
                                ln_stats(v, "d", L, B[L], B[L]["u"], "h_res")
                            for L in lanes:
                                ln_scale(v, "d", L, B[L])
                            for L in lanes:
                                b = B[L]
                                v.wait_ge(S("d_out"), L + 1)
                                V.tensor_tensor(rows4(b["v"][:]), rows4(b["v"][:]), each_row(gamma2), ALU.mult).then_inc(S("dg"), 1)
                            for L in lanes:
                                b = B[L]
                                v.wait_ge(S("dg"), L + 1)
                                v.wait_ge(S("x2b"), L + 1)
                                V.tensor_tensor(b["u"][:], b["v"][:], b["w"][:], ALU.add).then_inc(S("x3_pre"), 1)
                            for L in lanes:
                                ln_stats(v, "e", L, B[L], B[L]["u"], "x3_pre")
                            for L in lanes:
                                ln_scale(v, "e", L, B[L])
                        else:
                            for L in lanes:
                                b = B[L]
                                v.wait_ge(S("divided"), L + 1)
                                v.wait_ge(S("xo"), L + 1)
                                V.tensor_tensor(b["u"][:], b["o"][:], b["xo"][:], ALU.add).then_inc(S("x4_pre"), 1)
                            for L in lanes:
                                ln_stats(v, "f", L, B[L], B[L]["u"], "x4_pre")
                            for L in lanes:
                                ln_scale(v, "f", L, B[L])
                all_meet()
    ctx.close()


def kernel(**inputs):
    import numpy as np
    from concourse import bacc
    from concourse.bass_utils import run_bass_kernel_spmd

    def padded(a, n, value=0):
        a = np.ascontiguousarray(a)
        return np.concatenate([a, np.full((n - a.shape[0],) + a.shape[1:], value, a.dtype)])

    dst = np.asarray(inputs["dst"])
    arrays = {
        "x": padded(inputs["x"], NT),
        "src": padded(inputs["src"], ET),
        "dst": padded(np.concatenate([np.full((1,), -1, dst.dtype), dst]), ET + 2, NODES),
        "ea32": padded(inputs["edge_attr_32"], ET),
        "ea64": padded(inputs["edge_attr_64"], ET),
        "ew": padded(inputs["edge_weight"], ET).reshape(1, ET),
    }
    weights = {k: np.ascontiguousarray(v) for k, v in inputs.items() if k.startswith("L")}
    nc = bacc.Bacc("TRN2", target_bir_lowering=False, num_devices=1)

    def declare(name, a):
        return nc.dram_tensor(name, list(a.shape), mybir.dt.from_np(a.dtype), kind="ExternalInput").ap()

    edge = [declare(n, a) for n, a in arrays.items()]
    w = {n: declare(n, a) for n, a in weights.items()}
    out = nc.dram_tensor("out", [NT, D], F32, kind="ExternalOutput").ap()
    build(nc, *edge, w, out)
    r = run_bass_kernel_spmd(nc, [{**arrays, **weights}], core_ids=[0])
    return r.results[0]["out"][:NODES]
```

```python
from contextlib import ExitStack

import concourse.bass as bass
from concourse import mybir

F32 = mybir.dt.float32
I32 = mybir.dt.int32
U32 = mybir.dt.uint32
ALU = mybir.AluOpType
ACT = mybir.ActivationFunctionType
AX = mybir.AxisListType

P = 128
D = 128
SUB = 4
CH = P * SUB
NODES, EDGES = 50000, 25000
NL = 7
EL = 5
GL = 10
N_IT = -(-NODES // (CH * NL))
E_IT = -(-EDGES // (CH * EL))
NT = N_IT * NL * CH
ET = E_IT * EL * CH
TILES = ET // P
MAP_IT = (N_IT + 1) // 2
MAP_W = -(-TILES // MAP_IT)
READ_IT = N_IT - MAP_IT
MAP_R = -(-TILES // READ_IT)
COLS = max(MAP_W * MAP_IT, MAP_R * READ_IT, TILES + GL * SUB)
NODE_LAG, HOP0_LAG, GCN_LAG, GCN_LAST_LAG, HOP4_LAG, HOP5_LAG = 183, 171, 45, 52, 138, 137
FAR = 1000000
BIG = 3.0e38
EPS = 1e-5


def build(nc, x, src, dst, ea32, ea64, ew, w, out):
    ctx = ExitStack()

    def sb(name, shape, dt=F32):
        return ctx.enter_context(nc.sbuf_tensor(name, shape, dt))

    def dram(name, shape, dt=F32):
        return nc.dram_tensor(name, shape, dt, kind="Internal").ap()

    sems, handles = {}, []

    def S(name):
        if name not in sems:
            if len(sems) == len(handles):
                handles.append(ctx.enter_context(nc.semaphore(f"signal_{len(handles)}")))
            sems[name] = handles[len(sems)]
        return sems[name]

    pool_dma = {n: ctx.enter_context(nc.semaphore(n)) for n in
                ["edges", "map_written", "map_read"] + [f"gathered{L}" for L in range(GL)] + [f"scattered{L}" for L in range(EL)]}

    def new_phase():
        sems.clear()

    def all_meet():
        numbers = sorted(s.num for s in handles)
        assert numbers == list(range(numbers[0], numbers[0] + len(numbers)))
        nc.all_engine_barrier()
        nc.gpsimd.sem_clear(range(numbers[0], numbers[0] + len(numbers)))
        nc.all_engine_barrier()

    tables = [dram(f"table_{n}", [NT + ET, D]) for n in ("xw0", "xw1", "xw2", "x2", "x3")]
    x1_slots = dram("x1_slots", [ET, D])
    node_map = dram("node_map", [NT, 1], U32)
    pen_row = dram("pen_row", [1, ET])
    nst_row = dram("nst_row", [1, ET])
    cnt_row = dram("cnt_row", [1, ET])

    ident = sb("ident", [P, P])
    ones = sb("ones", [1, P])
    eps = sb("eps", [P, 1])
    W0 = sb("W0", [P, D])
    WI0 = sb("WI0", [P, D])
    WS = [None, sb("WS1", [P, D]), sb("WS2", [P, D])]
    src_rep, dst_rep, self_rep = (sb(n, [P, D]) for n in ("src_rep", "dst_rep", "self_rep"))
    xw0_bias_row = sb("xw0_bias_row", [1, D])
    h1_bias = sb("h1_bias", [P, 1])
    h2_bias = sb("h2_bias", [P, 1])
    bias0, gamma0, beta0 = (sb(n, [P, D]) for n in ("bias0", "gamma0", "beta0"))
    bs_row = [sb(f"bs_row{i}", [P, D]) for i in range(3)]
    Wq, Wk, Wv, Wo = (sb(n, [P, D]) for n in ("Wq", "Wk", "Wv", "Wo"))
    bq, bk, bv = (sb(n, [P, 1]) for n in ("bq", "bk", "bv"))
    bo, gamma2, beta2 = (sb(n, [P, D]) for n in ("bo", "gamma2", "beta2"))
    we2_rep = sb("we2_rep", [33, D])
    head_sum = sb("head_sum", [P, D])
    q3_rep, k3_rep, Wv3 = (sb(n, [P, D]) for n in ("q3_rep", "k3_rep", "Wv3"))
    we3_rep = sb("we3_rep", [65, D])
    bias3 = sb("bias3", [P, D])
    sel4, sel8 = sb("sel4", [P, 4]), sb("sel8", [P, 8])
    m_slot = sb("m_slot", [P, MAP_W], U32)
    src_idx = sb("src_idx", [P, COLS], U32)
    dst_idx = sb("dst_idx", [P, COLS], U32)
    end_idx = sb("end_idx", [P, COLS], U32)
    slot_idx = sb("slot_idx", [P, COLS], U32)
    own_idx = sb("own_idx", [P, COLS], U32)
    slot_no = sb("slot_no", [P, COLS], U32)
    dis = sb("dis", [P, COLS])

    ps = ctx.enter_context(nc.psum_tensor("ps", [P, 8, CH], F32))

    def rows4(t):
        return t.rearrange("p (j f) -> p j f", j=SUB)

    def each_row(row):
        return row[:, None, :].to_broadcast([P, SUB, D])

    def by_row(cols, width=D):
        return cols[:, :, None].to_broadcast([P, cols.shape[1], width])

    with ExitStack() as tmp:
        def tb(name, shape, dt=F32):
            return tmp.enter_context(nc.sbuf_tensor(name, shape, dt))

        H = TILES // 2
        edge_i = tb("edge_i", [H, 2, 4, P], I32)
        edge_f = tb("edge_f", [H, 2, 4, P])
        mark = tb("mark", [H, 2, 5, P])
        att = tb("att", [P, 2, D])
        prod = tb("prod", [P, 4, D])
        sums = tb("sums", [P, 6, 4])
        Win, WinT, Ws0 = tb("Win", [P, D]), tb("WinT", [P, D]), tb("Ws0", [P, D])
        b_in, bs0c = tb("b_in", [P, 1]), tb("bs0c", [P, 1])
        We2, We3 = tb("We2", [33, 8]), tb("We3", [64, D])
        We3s = tb("We3s", [65, 4])
        Wq3, Wk3 = tb("Wq3", [P, D]), tb("Wk3", [P, D])
        node_no = tb("node_no", [P, NT // P], U32)
        cnt_in = tb("cnt_in", [1, ET // 8])
        cnt_out = tb("cnt_out", [1, ET // 8])
        one_row = tb("one_row", [1, ET // 8])
        cnt_last = tb("cnt_last", [1, 1])
        deg_rows = tb("deg_rows", [H, 2, P])
        deg = tb("deg", [P, TILES])

        cols = [(b_in, w["L1_gnn_b_in"]), (bs0c, w["L1_gnn_bs"][0]), (h2_bias, w["L1_gnn_bs"][1]),
                (bq, w["L2_gnn_bq"]), (bk, w["L2_gnn_bk"]), (bv, w["L2_gnn_bv"])]
        rows = [(bias0, w["L0_gnn_bias"]), (gamma0, w["L0_gnn_gamma"]), (beta0, w["L0_gnn_beta"]),
                (bs_row[0], w["L1_gnn_bs"][0]), (bs_row[1], w["L1_gnn_bs"][1]),
                (bs_row[2], w["L1_gnn_bs"][2]), (bo, w["L2_gnn_bo"]),
                (gamma2, w["L2_gnn_gamma"]), (beta2, w["L2_gnn_beta"]), (bias3, w["L3_gnn_bias"]),
                (att[:, 0, :], w["L0_gnn_att_src"].rearrange("h c -> (h c)")),
                (att[:, 1, :], w["L0_gnn_att_dst"].rearrange("h c -> (h c)"))]
        mats = [(W0, w["L0_gnn_W"]), (Win, w["L1_gnn_W_in"]), (Ws0, w["L1_gnn_Ws"][0]),
                (WS[1], w["L1_gnn_Ws"][1]), (WS[2], w["L1_gnn_Ws"][2]),
                (Wq, w["L2_gnn_Wq"]), (Wk, w["L2_gnn_Wk"]), (Wv, w["L2_gnn_Wv"]), (Wo, w["L2_gnn_Wo"]),
                (Wv3, w["L3_gnn_Wv"]), (Wq3, w["L3_gnn_Wq"]), (Wk3, w["L3_gnn_Wk"]),
                (We3, w["L3_gnn_We"])]
        small = [(We2[0:32, :], w["L2_gnn_We"]), (We2[32:33, :], w["L2_gnn_be"][None, :]),
                 (We3s[64:65, :], w["L3_gnn_gate"][None, :])]
        loads = ([(c[:], a.rearrange("(p o) -> p o", o=1)) for c, a in cols]
                 + [(r[:, :], a[None, :].to_broadcast([P, D])) for r, a in rows]
                 + [(m[:], a) for m, a in mats] + small)
        edge_loads = [(edge_i[:, :, 0, :], src.rearrange("(h r c) -> r h c", h=2, c=P))] + [
            (edge_i[:, :, k, :], dst[o:o + ET].rearrange("(h r c) -> r h c", h=2, c=P))
            for k, o in ((1, 1), (2, 0), (3, 2))]

        with nc.Block() as block:
            @block.sync
            def _(sp):
                for to, of in loads:
                    sp.dma_start(to, of).then_inc(S("weights"), 16)
                sp.wait_ge(S("node_no"), 1)
                sp.dma_start(node_map.rearrange("(p c) o -> p (c o)", p=P), node_no[:]).then_inc(S("stored"), 16)
                sp.wait_ge(S("marks"), 2)
                for row, k in ((nst_row, 1), (pen_row, 2)):
                    sp.dma_start(row.rearrange("o (h r c) -> (o r) h c", h=2, c=P), mark[:, :, k, :]).then_inc(S("rows_stored"), 16)
                sp.wait_ge(S("rows_stored"), 32)
                for k in range(8):
                    if k:
                        sp.wait_ge(S("counted"), k)
                    piece = slice(k * (ET // 8), (k + 1) * (ET // 8))
                    sp.dma_start(cnt_in[:], nst_row[:, piece]).then_inc(S("cnt_loaded"), 16)
                    sp.wait_ge(S("counted"), k + 1)
                    sp.dma_start(cnt_row[:, piece], cnt_out[:]).then_inc(S("cnt_stored"), 16)
                    sp.wait_ge(S("cnt_stored"), 16 * (k + 1))
                sp.dma_start(deg_rows[:], cnt_row.rearrange("o (h r c) -> (o r) h c", h=2, c=P)).then_inc(S("deg_rows"), 16)
                sp.wait_ge(S("stored"), 16)

            @block.gpsimd
            def _(pool):
                for to, of in edge_loads:
                    pool.dma_start(to, of).then_inc(pool_dma["edges"], 16)
                nc.gpsimd.iota(node_no[:], pattern=[[1, NT // P]], base=0, channel_multiplier=NT // P).then_inc(S("node_no"), 1)
                nc.gpsimd.iota(slot_no[:], pattern=[[P, COLS]], base=NT, channel_multiplier=1).then_inc(S("slot_no"), 1)
                nc.gpsimd.memset(src_idx[:], 0).then_inc(S("zeros"), 1)
                nc.gpsimd.memset(dst_idx[:], 0).then_inc(S("zeros"), 1)
                nc.gpsimd.memset(end_idx[:], FAR).then_inc(S("zeros"), 1)
                nc.gpsimd.memset(slot_idx[:], 0).then_inc(S("zeros"), 1)
                nc.gpsimd.memset(own_idx[:], 0).then_inc(S("zeros"), 1)
                nc.gpsimd.memset(dis[:], 0.0).then_inc(S("zeros"), 1)
                nc.gpsimd.memset(ones[:], 1.0).then_inc(S("zeros"), 1)
                nc.gpsimd.memset(eps[:], EPS).then_inc(S("zeros"), 1)
                for t in (ident, sel4, sel8):
                    nc.gpsimd.memset(t[:], 0.0).then_inc(S("cleared"), 1)
                nc.gpsimd.memset(head_sum[:], 0.25).then_inc(S("cleared"), 1)
                pool.wait_ge(S("cleared"), 4)
                for t, n in ((ident, 1), (sel4, 32), (sel8, 16)):
                    nc.gpsimd.affine_select(out=t[:], in_=t[:], compare_op=ALU.not_equal, fill=1.0, base=0,
                                            pattern=[[-n, t.shape[1]]], channel_multiplier=1).then_inc(S("masks"), 1)
                hs = head_sum.rearrange("p (h c) -> p h c", h=8)
                nc.gpsimd.affine_select(out=hs, in_=hs, compare_op=ALU.is_ge, fill=0.0, base=0,
                                        pattern=[[-16, 8], [0, 16]], channel_multiplier=1).then_inc(S("masks"), 1)
                pool.wait_ge(S("masks"), 4)
                nc.gpsimd.affine_select(out=hs, in_=hs, compare_op=ALU.is_ge, fill=0.0, base=15,
                                        pattern=[[16, 8], [0, 16]], channel_multiplier=-1).then_inc(S("masks"), 1)

            @block.tensor
            def _(pe):
                pe.wait_ge(S("masks"), 5)
                pe.wait_ge(S("zeros"), 8)
                pe.wait_ge(S("weights"), 16 * len(loads))
                nc.tensor.transpose(ps[:, 0, 0:P], Win[:], ident[:]).then_inc(S("win_ps"), 1)
                pe.wait_ge(S("winT"), 1)
                nc.tensor.matmul(ps[:, 0, 128:256], WinT[:], Ws0[:], start=True, stop=True).then_inc(S("wi0_ps"), 1)
                nc.tensor.matmul(ps[0:1, 0, 256:384], b_in[:], Ws0[:], start=True, stop=True).then_inc(S("wi0_ps"), 1)
                nc.tensor.matmul(ps[:, 0, 384:385], Ws0[:], b_in[:], start=True, stop=True).then_inc(S("wi0_ps"), 1)
                pe.wait_ge(S("marks"), 2)
                for h in range(2):
                    for k, t in enumerate((edge_f[:, h, 0, :], edge_f[:, h, 1, :], mark[:, h, 3, :])):
                        nc.tensor.transpose(ps[:, 1 + k, h * H:(h + 1) * H], t, ident[0:H, 0:H]).then_inc(S("cols_ps"), 1)
                pe.wait_ge(S("deg_rows"), 16)
                for h in range(2):
                    nc.tensor.transpose(ps[:, 4, h * H:(h + 1) * H], deg_rows[:, h, :], ident[0:H, 0:H]).then_inc(S("deg_ps"), 1)

            @block.scalar
            def _(act):
                act.wait_ge(S("deg_ps"), 2)
                nc.scalar.activation(deg[:], ps[:, 4, 0:TILES], ACT.Sqrt, bias=1.0).then_inc(S("deg"), 1)

            @block.vector
            def _(v):
                V = nc.vector
                v.wait_ge(pool_dma["edges"], 64)
                V.tensor_copy(edge_f[:], edge_i[:]).then_inc(S("edges_f"), 1)
                v.wait_ge(S("edges_f"), 1)
                V.tensor_tensor(mark[:, :, 0, :], edge_f[:, :, 1, :], edge_f[:, :, 3, :], ALU.is_equal).then_inc(S("m"), 1)
                V.tensor_tensor(mark[:, :, 1, :], edge_f[:, :, 1, :], edge_f[:, :, 2, :], ALU.is_equal).then_inc(S("m"), 1)
                v.wait_ge(S("m"), 2)
                V.tensor_scalar(mark[:, :, 4, :], mark[:, :, 0, :], float(FAR), None, ALU.mult).then_inc(S("m"), 1)
                V.tensor_scalar(mark[:, :, 2, :], mark[:, :, 1, :], 0.5, 2 * BIG / 2, ALU.subtract, ALU.mult).then_inc(S("marks"), 1)
                v.wait_ge(S("m"), 3)
                V.tensor_tensor(mark[:, :, 3, :], mark[:, :, 4, :], edge_f[:, :, 1, :], ALU.add).then_inc(S("marks"), 1)
                v.wait_ge(S("win_ps"), 1)
                V.tensor_copy(WinT[:], ps[:, 0, 0:P]).then_inc(S("winT"), 1)
                v.wait_ge(S("wi0_ps"), 3)
                V.tensor_copy(WI0[:], ps[:, 0, 128:256])
                V.tensor_copy(xw0_bias_row[:], ps[0:1, 0, 256:384])
                V.tensor_tensor(h1_bias[:], ps[:, 0, 384:385], bs0c[:], ALU.add)
                V.tensor_tensor(prod[:, 0, :], W0[:], att[:, 0, :], ALU.mult).then_inc(S("prod"), 1)
                V.tensor_tensor(prod[:, 1, :], W0[:], att[:, 1, :], ALU.mult).then_inc(S("prod"), 1)
                v.wait_ge(S("prod"), 2)
                for k, t in enumerate((prod[:, 0, :], prod[:, 1, :], Wq3[:], Wk3[:])):
                    V.tensor_reduce(sums[:, k, :], t.rearrange("p (h c) -> p h c", h=4), AX.X, ALU.add).then_inc(S("sums"), 1)
                V.tensor_reduce(We3s[0:64, :], We3[:].rearrange("p (h c) -> p h c", h=4), AX.X, ALU.add).then_inc(S("sums"), 1)
                v.wait_ge(S("sums"), 5)
                for k, t in enumerate((src_rep, dst_rep, q3_rep, k3_rep)):
                    V.tensor_copy(t.rearrange("p (h c) -> p h c", h=4), by_row(sums[:, k, :], 32)).then_inc(S("rep"), 1)
                V.tensor_copy(we3_rep[0:64, :].rearrange("p (h c) -> p h c", h=4),
                              We3s[0:64, :, None].to_broadcast([64, 4, 32]))
                V.tensor_scalar(we3_rep[64:65, :].rearrange("p (h c) -> p h c", h=4),
                                We3s[64:65, :, None].to_broadcast([1, 4, 32]), float(32.0 ** 0.5), None, ALU.mult)
                V.tensor_copy(we2_rep.rearrange("p (h c) -> p h c", h=8), We2[:, :, None].to_broadcast([33, 8, 16]))
                v.wait_ge(S("rep"), 4)
                V.tensor_tensor(self_rep[:], src_rep[:], dst_rep[:], ALU.add)
                v.wait_ge(S("cols_ps"), 6)
                v.wait_ge(S("zeros"), 8)
                V.tensor_copy(src_idx[:, 0:TILES], ps[:, 1, 0:TILES])
                V.tensor_copy(dst_idx[:, 0:TILES], ps[:, 2, 0:TILES])
                V.tensor_copy(end_idx[:, 0:TILES], ps[:, 3, 0:TILES])
                V.memset(one_row[:], 1.0).then_inc(S("cnt_init"), 1)
                V.memset(cnt_last[:], 0.0).then_inc(S("cnt_init"), 1)
                for k in range(8):
                    v.wait_ge(S("cnt_init"), 2 + k)
                    v.wait_ge(S("cnt_loaded"), 16 * (k + 1))
                    if k:
                        v.wait_ge(S("cnt_stored"), 16 * k)
                    V.tensor_tensor_scan(cnt_out[:], cnt_in[:], one_row[:], cnt_last[:], ALU.mult, ALU.add).then_inc(S("counted"), 1)
                    v.wait_ge(S("counted"), k + 1)
                    V.tensor_copy(cnt_last[:], cnt_out[:, ET // 8 - 1:ET // 8]).then_inc(S("cnt_init"), 1)
                v.wait_ge(S("deg"), 1)
                V.reciprocal(dis[:, 0:TILES], deg[:])
        all_meet()

    class Turn:
        def __init__(self, plan, n, lag, it, new, old):
            self.n, self.lag, self.it, self.runs = n, lag, it, (new, old)
            self.place = {step: place for step, (place, _) in plan.items()}
            self.at = {name: place for place, names in plan.values() for name in names.split()}
            assert max(self.place.values()) <= n * lag
            self.first = not old
            self.steps, self.now, self.issued = [], None, []

        def __call__(self, name):
            def add(step):
                self.steps.append((self.place[name], step))
                return step
            return add

        def run(self):
            period, order = self.n * self.lag, []
            for k, (place, step) in enumerate(self.steps):
                for L in range(self.n):
                    late, when = divmod(place + self.lag * L, period)
                    if self.runs[late]:
                        order.append((when, k, L, late, place, step))
            for when, k, L, late, place, step in sorted(order, key=lambda o: o[:3]):
                self.now = place
                step(L, self.it - late if late else self.it)
            self.steps = []

        def count(self, name, L, back):
            period, place = self.n * self.lag, self.at[name]
            then, now = place + self.lag * (L - back), self.now + self.lag * L
            assert then <= now, (name, then, now)
            turn = now // period
            if then // period != turn or (self.first and L < back):
                return None
            since = -((place - turn * period) // self.lag)
            if self.first:
                since = max(since, 0)
            return L - back - since + 1

        def due(self, eng, name, L, back=0, each=1):
            n = self.count(name, L, back)
            if n is not None:
                eng.wait_ge(S(name), n * each)

        def due_dma(self, eng, name, L, back=0):
            if self.count(name, L, back) is not None:
                eng.wait_ge(S(f"{name}{(L - back) % self.n}"), 16)

        def issue(self, name, L):
            self.issued.append(S(f"{name}{L}"))
            return self.issued[-1]

        def end_dmas(self, eng):
            for sem in self.issued:
                eng.wait_ge(sem, 16)

    def turns(n_it, turn_of):
        turn_of(0, True, False)
        with nc.Fori(1, n_it) as it:
            turn_of(it, True, True)
        turn_of(n_it, False, True)

    def ln_plan(n, stats, root, scale, apply):
        return {n + ".stats": (stats, f"{n}_st {n}_mv"), n + ".root": (root, n + "_sd"),
                n + ".scale": (scale, f"{n}_rs {n}_nm"), n + ".apply": (apply, n + "_out")}

    def ln_stats(v, c, n, L, b, t, ready):
        c.due(v, ready, L)
        for j in range(SUB):
            nc.vector.bn_stats(b["st"][:, 6 * j:6 * j + 6], t[:, j * D:(j + 1) * D]).then_inc(S(n + "_st"), 1)
        c.due(v, n + "_st", L, each=SUB)
        for j in range(SUB):
            nc.vector.bn_aggr(b["mv"][:, 2 * j:2 * j + 2], b["st"][:, 6 * j:6 * j + 6]).then_inc(S(n + "_mv"), 1)

    def ln_root(act, c, n, L, b):
        c.due(act, n + "_mv", L, each=SUB)
        var = b["mv"].rearrange("p (j t) -> p j t", t=2)[:, :, 1]
        nc.scalar.activation(b["sd"][:], var, ACT.Sqrt, bias=eps[:, 0:1]).then_inc(S(n + "_sd"), 1)

    def ln_scale(v, c, n, L, b):
        c.due(v, n + "_sd", L)
        nc.vector.reciprocal(b["rs"][:], b["sd"][:]).then_inc(S(n + "_rs"), 1)
        c.due(v, n + "_rs", L)
        mean = b["mv"].rearrange("p (j t) -> p j t", t=2)[:, :, 0]
        nc.vector.scalar_tensor_tensor(out=b["nm"][:], in0=mean, scalar=-1.0, in1=b["rs"][:],
                                       op0=ALU.mult, op1=ALU.mult).then_inc(S(n + "_nm"), 1)

    def ln_apply(act, c, n, L, b, to, t):
        c.due(act, n + "_nm", L)
        for j in range(SUB):
            last = nc.scalar.activation(to[:, j * D:(j + 1) * D], t[:, j * D:(j + 1) * D], ACT.Identity,
                                        scale=b["rs"][:, j:j + 1], bias=b["nm"][:, j:j + 1])
        last.then_inc(S(n + "_out"), 1)

    def ln_act(act, step, B, n, to, of):
        @step(n + ".root")
        def _(L, i):
            ln_root(act, step, n, L, B[L])

        @step(n + ".apply")
        def _(L, i):
            ln_apply(act, step, n, L, B[L], B[L][to], B[L][of])

    def ln_vector(v, step, B, n, of, ready):
        @step(n + ".stats")
        def _(L, i):
            ln_stats(v, step, n, L, B[L], B[L][of], ready)

        @step(n + ".scale")
        def _(L, i):
            ln_scale(v, step, n, L, B[L])

    def turn(pe, to, t, width=P):
        for j in range(SUB):
            last = nc.tensor.transpose(to[0:width, j * P:(j + 1) * P], t[:, j * width:(j + 1) * width], ident[:])
        return last

    def rows_times(pe, to, tT, W, bias_row=None):
        for j in range(SUB):
            last = nc.tensor.matmul(to[:, j * D:(j + 1) * D], tT[:, j * P:(j + 1) * P], W[:],
                                    start=True, stop=bias_row is None)
            if bias_row is not None:
                last = nc.tensor.matmul(to[:, j * D:(j + 1) * D], ones[:], bias_row[:], start=False, stop=True)
        return last

    def lane_buffers(stack, tag, names):
        b = {n: stack.enter_context(nc.sbuf_tensor(f"{n}_{tag}", [P, CH], F32)) for n in names.split()}
        for n, width in (("st", 6 * SUB), ("mv", 2 * SUB), ("sd", SUB), ("rs", SUB), ("nm", SUB)):
            b[n] = stack.enter_context(nc.sbuf_tensor(f"{n}_{tag}", [P, width], F32))
        return b

    def node_rows(table, i, L):
        return table[bass.ds((i * NL + L) * CH, CH), :].rearrange("(p j) f -> p (j f)", j=SUB)

    def write_begin(pool, it, m_idx):
        nc.gpsimd.tensor_copy(m_idx[:, 0:MAP_W], end_idx[:, bass.ds(it * MAP_W, MAP_W)]).then_inc(S("m_idx"), 1)
        nc.gpsimd.tensor_copy(m_slot[:], slot_no[:, bass.ds(it * MAP_W, MAP_W)]).then_inc(S("m_idx"), 1)
        pool.wait_ge(S("m_idx"), 2)

    def write_part(pool, m_idx, m_val, L):
        for t in range(L * MAP_W // NL, (L + 1) * MAP_W // NL):
            pool.indirect_dma_start(out=node_map, out_offset=bass.IndirectOffsetOnAxis(ap=m_idx[:, t:t + 1], axis=0),
                                    in_=m_slot[:, t:t + 1], in_offset=None,
                                    bounds_check=NT - 1, oob_is_err=False).then_inc(pool_dma["map_written"], 16)

    def write_end(pool, it, m_val):
        pool.wait_ge(pool_dma["map_written"], (it + 1) * (16 * MAP_W))

    def read_begin(pool, it, m_idx):
        for k, of in enumerate((src_idx, dst_idx)):
            nc.gpsimd.tensor_copy(m_idx[:, k * MAP_R:(k + 1) * MAP_R], of[:, bass.ds((it - MAP_IT) * MAP_R, MAP_R)]).then_inc(S("m_idx"), 1)
        pool.wait_ge(S("m_idx"), 2)

    def read_part(pool, m_idx, m_val, L):
        for t in range(L * 2 * MAP_R // NL, (L + 1) * 2 * MAP_R // NL):
            pool.indirect_dma_start(out=m_val[:, t:t + 1], out_offset=None, in_=node_map,
                                    in_offset=bass.IndirectOffsetOnAxis(ap=m_idx[:, t:t + 1], axis=0),
                                    bounds_check=NT - 1, oob_is_err=False).then_inc(pool_dma["map_read"], 16)

    def read_end(pool, it, m_val):
        pool.wait_ge(pool_dma["map_read"], (it - (MAP_IT - 1)) * (16 * 2 * MAP_R))
        for k, to in enumerate((slot_idx, own_idx)):
            nc.gpsimd.tensor_copy(to[:, bass.ds((it - MAP_IT) * MAP_R, MAP_R)], m_val[:, k * MAP_R:(k + 1) * MAP_R])

    node_plan = {
        "map": (0, ""), "load": (40, "x_in"), "turn_x": (72, "xT_ps"), "copy_xT": (83, "xT"), "rows_h": (90, "h_ps"),
        "x_beta": (110, "xb xxb"), "gelu": (142, "gelu"), **ln_plan("a", 221, 237, 242, 248), "x1_pre": (266, "ag x1_pre"),
        **ln_plan("b", 282, 298, 302, 308), "turn_x1": (326, "x1T_ps"), "copy_x1T": (356, "x1T"),
        "times_WI": (364, "h1_ps"), "relu_h1": (375, "h1T"), "rows_xw0": (379, "xw0_ps"), "copy_xw0": (399, "xw0"),
        "store_xw0": (408, "xw0_stored"), "times_W1": (410, "h2_ps"), "rows_xw1": (419, "xw1_ps"), "relu_h2": (422, "h2T"),
        "rows_xw2": (447, "xw2_ps"), "copy_xw1": (454, "xw1"), "copy_xw2": (459, "xw2"), "store_xw1": (462, "xw1_stored"),
        "store_xw2": (468, "xw2_stored"), "x2_pre": (488, "h3_pre x2_pre"), **ln_plan("c", 504, 544, 548, 564),
        "store_x2": (582, "x2_stored"), "h_res": (601, "h_res"), **ln_plan("d", 611, 630, 663, 770), "x2_beta": (685, "x2b"),
        "x3_pre": (884, "dg x3_pre"), **ln_plan("e", 917, 946, 991, 1013), "store_x3": (1031, "x3_stored"),
        "x4_pre": (1064, "x4_pre"), **ln_plan("f", 1081, 1097, 1114, 1120), "store_out": (1135, "out_stored")}

    new_phase()
    with ExitStack() as tmp:
        B = [lane_buffers(tmp, f"n{L}", "x u v w x1 x1T h1T xw0 xw1 xw2 x2") for L in range(NL)]
        for b in B:
            b["x3"], b["x4"] = b["x"], b["x1"]
        m_idx = tmp.enter_context(nc.sbuf_tensor("m_idx", [P, max(MAP_W, 2 * MAP_R)], U32))
        m_val = tmp.enter_context(nc.sbuf_tensor("m_val", [P, max(MAP_W, 2 * MAP_R)], U32))
        X, HH, X1T, XW0, H1, XW1, H2, XW2 = (ps[:, k, :] for k in range(8))

        def node_turn(it, new, old, map_begin, map_part, map_end):
            with nc.Block() as block:
                @block.sync
                def _(sp):
                    step = Turn(node_plan, NL, NODE_LAG, it, new, old)

                    @step("load")
                    def _(L, i):
                        for n in ("xw0", "xw1", "xw2", "x2", "x3", "out"):
                            step.due_dma(sp, n + "_stored", L, NL)
                        sp.dma_start(B[L]["x"][:], node_rows(x, i, L)).then_inc(step.issue("x_in", L), 16)

                    def store(n, table, name, ready):
                        @step("store_" + n)
                        def _(L, i):
                            step.due(sp, ready, L)
                            sp.dma_start(node_rows(table, i, L), B[L][name][:]).then_inc(step.issue(n + "_stored", L), 16)

                    store("xw0", tables[0], "xw0", "xw0")
                    store("xw1", tables[1], "xw1", "xw1")
                    store("xw2", tables[2], "xw2", "xw2")
                    store("x2", tables[3], "x2", "c_out")
                    store("x3", tables[4], "x3", "e_out")
                    store("out", out, "x4", "f_out")
                    step.run()
                    step.end_dmas(sp)

                @block.gpsimd
                def _(pool):
                    step = Turn(node_plan, NL, NODE_LAG, it, new, old)
                    if new:
                        map_begin(pool, it, m_idx)

                    @step("map")
                    def _(L, i):
                        map_part(pool, m_idx, m_val, L)

                    @step("x_beta")
                    def _(L, i):
                        b = B[L]
                        step.due_dma(pool, "x_in", L)
                        nc.gpsimd.tensor_tensor(rows4(b["w"][:]), rows4(b["x"][:]), each_row(beta0), ALU.add).then_inc(S("xb"), 1)
                        step.due(pool, "xb", L)
                        nc.gpsimd.tensor_tensor(b["w"][:], b["w"][:], b["x"][:], ALU.add).then_inc(S("xxb"), 1)

                    @step("x2_beta")
                    def _(L, i):
                        b = B[L]
                        step.due(pool, "c_out", L)
                        nc.gpsimd.tensor_tensor(rows4(b["w"][:]), rows4(b["x2"][:]), each_row(beta2), ALU.add).then_inc(S("x2b"), 1)

                    @step("x4_pre")
                    def _(L, i):
                        b = B[L]
                        step.due(pool, "e_out", L)
                        nc.gpsimd.tensor_tensor(rows4(b["v"][:]), rows4(b["x3"][:]), each_row(bias3), ALU.add).then_inc(S("x4_pre"), 1)

                    step.run()
                    if new:
                        map_end(pool, it, m_val)

                @block.tensor
                def _(pe):
                    step = Turn(node_plan, NL, NODE_LAG, it, new, old)

                    @step("turn_x")
                    def _(L, i):
                        step.due_dma(pe, "x_in", L)
                        step.due(pe, "xT", L, 1)
                        turn(pe, X, B[L]["x"]).then_inc(S("xT_ps"), 1)

                    @step("rows_h")
                    def _(L, i):
                        step.due(pe, "xT", L)
                        step.due(pe, "gelu", L, 1)
                        rows_times(pe, HH, B[L]["x1T"], W0, bias0[0:1, :]).then_inc(S("h_ps"), 1)

                    @step("turn_x1")
                    def _(L, i):
                        step.due(pe, "b_out", L)
                        step.due(pe, "x1T", L, 1)
                        turn(pe, X1T, B[L]["x1"]).then_inc(S("x1T_ps"), 1)

                    @step("times_WI")
                    def _(L, i):
                        step.due(pe, "x1T", L)
                        step.due(pe, "h1T", L, 1)
                        nc.tensor.matmul(H1, WI0[:], B[L]["x1T"][:], start=True, stop=True).then_inc(S("h1_ps"), 1)

                    @step("rows_xw0")
                    def _(L, i):
                        step.due(pe, "xw0", L, 1)
                        rows_times(pe, XW0, B[L]["x1T"], WI0, xw0_bias_row).then_inc(S("xw0_ps"), 1)

                    @step("times_W1")
                    def _(L, i):
                        step.due(pe, "h1T", L)
                        step.due(pe, "h2T", L, 1)
                        nc.tensor.matmul(H2, WS[1][:], B[L]["h1T"][:], start=True, stop=True).then_inc(S("h2_ps"), 1)

                    @step("rows_xw1")
                    def _(L, i):
                        step.due(pe, "xw1", L, 1)
                        rows_times(pe, XW1, B[L]["h1T"], WS[1]).then_inc(S("xw1_ps"), 1)

                    @step("rows_xw2")
                    def _(L, i):
                        step.due(pe, "h2T", L)
                        step.due(pe, "xw2", L, 1)
                        rows_times(pe, XW2, B[L]["x1T"], WS[2]).then_inc(S("xw2_ps"), 1)

                    step.run()

                @block.scalar
                def _(act):
                    step = Turn(node_plan, NL, NODE_LAG, it, new, old)

                    @step("copy_xT")
                    def _(L, i):
                        step.due(act, "xT_ps", L)
                        nc.scalar.copy(B[L]["x1T"][:], X).then_inc(S("xT"), 1)

                    @step("gelu")
                    def _(L, i):
                        step.due(act, "h_ps", L)
                        nc.scalar.activation(B[L]["v"][:], HH, ACT.Gelu).then_inc(S("gelu"), 1)

                    ln_act(act, step, B, "a", "u", "v")
                    ln_act(act, step, B, "b", "x1", "v")

                    @step("copy_x1T")
                    def _(L, i):
                        step.due(act, "x1T_ps", L)
                        nc.scalar.copy(B[L]["x1T"][:], X1T).then_inc(S("x1T"), 1)

                    @step("relu_h1")
                    def _(L, i):
                        step.due(act, "h1_ps", L)
                        nc.scalar.activation(B[L]["h1T"][:], H1, ACT.Relu, bias=h1_bias[:, 0:1]).then_inc(S("h1T"), 1)

                    @step("copy_xw0")
                    def _(L, i):
                        step.due(act, "xw0_ps", L)
                        nc.scalar.copy(B[L]["xw0"][:], XW0).then_inc(S("xw0"), 1)

                    @step("relu_h2")
                    def _(L, i):
                        step.due(act, "xw0_ps", L)
                        step.due(act, "h2_ps", L)
                        nc.scalar.activation(B[L]["x1T"][:], H2, ACT.Relu, bias=h2_bias[:, 0:1]).then_inc(S("h2T"), 1)

                    @step("copy_xw1")
                    def _(L, i):
                        step.due(act, "xw1_ps", L)
                        nc.scalar.copy(B[L]["xw1"][:], XW1).then_inc(S("xw1"), 1)

                    @step("copy_xw2")
                    def _(L, i):
                        step.due(act, "xw2_ps", L)
                        nc.scalar.copy(B[L]["xw2"][:], XW2).then_inc(S("xw2"), 1)

                    ln_act(act, step, B, "c", "x2", "v")
                    ln_act(act, step, B, "d", "v", "u")
                    ln_act(act, step, B, "e", "x3", "u")

                    @step("f.root")
                    def _(L, i):
                        ln_root(act, step, "f", L, B[L])

                    step.run()

                @block.vector
                def _(v):
                    V = nc.vector
                    step = Turn(node_plan, NL, NODE_LAG, it, new, old)
                    ln_vector(v, step, B, "a", "v", "gelu")

                    @step("x1_pre")
                    def _(L, i):
                        b = B[L]
                        step.due(v, "a_out", L)
                        V.tensor_tensor(rows4(b["u"][:]), rows4(b["u"][:]), each_row(gamma0), ALU.mult).then_inc(S("ag"), 1)
                        step.due(v, "ag", L)
                        step.due(v, "xxb", L)
                        V.tensor_tensor(b["v"][:], b["u"][:], b["w"][:], ALU.add).then_inc(S("x1_pre"), 1)

                    ln_vector(v, step, B, "b", "v", "x1_pre")

                    @step("x2_pre")
                    def _(L, i):
                        b = B[L]
                        step.due(v, "xw2", L)
                        V.tensor_tensor(rows4(b["u"][:]), rows4(b["xw2"][:]), each_row(bs_row[2]), ALU.add).then_inc(S("h3_pre"), 1)
                        step.due(v, "h3_pre", L)
                        V.scalar_tensor_tensor(out=b["v"][:], in0=b["u"][:], scalar=0.0, in1=b["x1"][:],
                                               op0=ALU.max, op1=ALU.add).then_inc(S("x2_pre"), 1)

                    ln_vector(v, step, B, "c", "v", "x2_pre")

                    @step("h_res")
                    def _(L, i):
                        b = B[L]
                        step.due(v, "c_out", L)
                        V.tensor_tensor(rows4(b["u"][:]), rows4(b["x2"][:]), each_row(bo), ALU.add).then_inc(S("h_res"), 1)

                    ln_vector(v, step, B, "d", "u", "h_res")

                    @step("x3_pre")
                    def _(L, i):
                        b = B[L]
                        step.due(v, "d_out", L)
                        V.tensor_tensor(rows4(b["v"][:]), rows4(b["v"][:]), each_row(gamma2), ALU.mult).then_inc(S("dg"), 1)
                        step.due(v, "dg", L)
                        step.due(v, "x2b", L)
                        V.tensor_tensor(b["u"][:], b["v"][:], b["w"][:], ALU.add).then_inc(S("x3_pre"), 1)

                    ln_vector(v, step, B, "e", "u", "x3_pre")
                    ln_vector(v, step, B, "f", "v", "x4_pre")

                    @step("f.apply")
                    def _(L, i):
                        b = B[L]
                        step.due(v, "f_rs", L)
                        for j in range(SUB):
                            last = V.tensor_scalar(b["x4"][:, j * D:(j + 1) * D], b["v"][:, j * D:(j + 1) * D],
                                                   b["mv"][:, 2 * j:2 * j + 1], b["rs"][:, j:j + 1], ALU.subtract, ALU.mult)
                        last.then_inc(S("f_out"), 1)

                    step.run()
            all_meet()

        write, read = (write_begin, write_part, write_end), (read_begin, read_part, read_end)
        node_turn(0, True, False, *write)
        with nc.Fori(1, MAP_IT) as it:
            node_turn(it, True, True, *write)
        with nc.Fori(MAP_IT, N_IT) as it:
            node_turn(it, True, True, *read)
        node_turn(N_IT, False, True, *read)

    arrived = [0] * GL

    class Hop:

        def __init__(self, stack, tag, plan, n, lag, names, gathers, maximum=True):
            self.plan, self.n, self.lag, self.n_it = plan, n, lag, ET // (CH * n)
            self.B = [lane_buffers(stack, f"{tag}_{L}", names) for L in range(n)]
            for L, b in enumerate(self.B):
                if maximum:
                    b["M"] = stack.enter_context(nc.sbuf_tensor(f"M_{tag}_{L}", [P, CH + 1], F32))
                    b["dn"] = stack.enter_context(nc.sbuf_tensor(f"dn_{tag}_{L}", [P, 32], F32))
                    b["rd"] = stack.enter_context(nc.sbuf_tensor(f"rd_{tag}_{L}", [P, 32], F32))
                b["dis"] = stack.enter_context(nc.sbuf_tensor(f"dis_{tag}_{L}", [P, SUB], F32))
                for g in gathers:
                    b[g] = stack.enter_context(nc.sbuf_tensor(f"{g}_{tag}_{L}", [P, CH], F32))
                    b["idx_" + g] = stack.enter_context(nc.sbuf_tensor(f"idx_{tag}_{g}_{L}", [P, SUB], U32))
            self.gathers, self.per = gathers, 16 * SUB * len(gathers)

        def steps(self, it, new, old):
            return Turn(self.plan, self.n, self.lag, it, new, old)

        def tiles(self, i, L):
            return bass.ds((i * self.n + L) * SUB, SUB)

        def rows(self, table, i, L, base=NT):
            return table[bass.ds(base + (i * self.n + L) * CH, CH), :].rearrange("(j p) f -> p j f", p=P)

        def cols(self, row, i, L, parts=P):
            return row[:, bass.ds((i * self.n + L) * CH, CH)].to_broadcast([parts, CH])

        def gather(self, pool, step, i, L, copied):
            b = self.B[L]
            for g, (table, rows, idx) in self.gathers.items():
                nc.gpsimd.tensor_copy(b["idx_" + g][:], idx[:, self.tiles(i, L)]).then_inc(S(copied), 1)
            step.due(pool, copied, L, each=len(self.gathers))
            for g, (table, rows, idx) in self.gathers.items():
                for t in range(SUB):
                    pool.indirect_dma_start(out=b[g][:, t * D:(t + 1) * D], out_offset=None, in_=table,
                                            in_offset=bass.IndirectOffsetOnAxis(ap=b["idx_" + g][:, t:t + 1], axis=0),
                                            bounds_check=rows - 1, oob_is_err=False).then_inc(pool_dma[f"gathered{L}"], 16)

        def gather_steps(self, pool, step, read):
            if step.first:
                @step("gather_first")
                def _(L, i):
                    self.gather(pool, step, i, L, "first_idx")

            @step("gather")
            def _(L, i):
                for name in read:
                    step.due(pool, name, L)
                self.gather(pool, step, i + 1, L, "next_idx")

        def due_gathered(self, eng, i, L):
            eng.wait_ge(pool_dma[f"gathered{L}"], (i + 1) * self.per + arrived[L])

        def end_gathers(self, pool):
            for L in range(self.n):
                arrived[L] += (self.n_it + 1) * self.per
                pool.wait_ge(pool_dma[f"gathered{L}"], arrived[L])

        def before(self, L):
            return self.B[(L - 1) % self.n]

        def no_sums(self, v, *names):
            for n in names:
                nc.vector.memset(self.before(0)[n][:], 0.0).then_inc(S("no_sums"), 1)
            v.wait_ge(S("no_sums"), len(names))

    def run_maximum(v, step, hop, L, score, limit, ready):
        V = nc.vector
        b, before = hop.B[L], hop.before(L)
        step.due(v, ready, L)
        step.due_dma(v, "pen_in", L)
        step.due(v, "M", L, 1)
        V.tensor_copy(b["M"][:, 0:1], before["M"][:, CH:CH + 1]).then_inc(S("M_first"), 1)
        step.due(v, "M_first", L)
        V.tensor_tensor_scan(b["M"][:, 1:CH + 1], b["pen"][:], limit, b["M"][:, 0:1], ALU.min, ALU.max).then_inc(S("M"), 1)
        step.due(v, "M", L)
        V.tensor_tensor(b["p"][:], score, b["M"][:, 1:CH + 1], ALU.subtract).then_inc(S("dz"), 1)
        V.tensor_tensor(b["F"][:], b["pen"][:], b["M"][:, 0:CH], ALU.min).then_inc(S("Dm0"), 1)
        step.due(v, "Dm0", L)
        V.tensor_tensor(b["F"][:], b["F"][:], b["M"][:, 1:CH + 1], ALU.subtract).then_inc(S("Dm"), 1)

    def run_weights(act, step, b, L):
        step.due(act, "dz", L)
        nc.scalar.activation(b["p"][:], b["p"][:], ACT.Exp).then_inc(S("p"), 1)
        step.due(act, "Dm", L)
        nc.scalar.activation(b["F"][:], b["F"][:], ACT.Exp).then_inc(S("F"), 1)

    def run_sums(v, step, hop, L, value, bias, ready):
        V = nc.vector
        b, before = hop.B[L], hop.before(L)
        step.due(v, "p", L)
        step.due(v, ready, L)
        V.scalar_tensor_tensor(out=b["msg"][:], in0=value, scalar=bias, in1=b["p"][:],
                               op0=ALU.add, op1=ALU.mult).then_inc(S("msg"), 1)
        step.due(v, "F", L)
        step.due(v, "den", L, 1)
        V.tensor_tensor_scan(b["den"][:], b["F"][:], b["p"][:], before["den"][:, CH - 1:CH], ALU.mult, ALU.add).then_inc(S("den"), 1)
        step.due(v, "msg", L)
        step.due(v, "num", L, 1)
        V.tensor_tensor_scan(b["num"][:], b["F"][:], b["msg"][:], before["num"][:, CH - 1:CH], ALU.mult, ALU.add).then_inc(S("num"), 1)

    def den_rows(pe, to, den, sel, heads):
        for j in range(SUB):
            last = nc.tensor.matmul(to[:, j * heads:(j + 1) * heads], den[:, j * P:(j + 1) * P], sel[:], start=True, stop=True)
        return last

    def divide(v, step, b, L, num_rows, den_r, heads, eps_den, to):
        V = nc.vector
        n = SUB * heads
        step.due(v, "num_rows", L)
        V.tensor_scalar(b["dn"][:, 0:n], den_r[:, 0:n], eps_den, None, ALU.add).then_inc(S("dn"), 1)
        step.due(v, "dn", L)
        V.reciprocal(b["rd"][:, 0:n], b["dn"][:, 0:n]).then_inc(S("rd"), 1)
        step.due(v, "rd", L)
        c = D // heads
        V.tensor_tensor(to.rearrange("p (n c) -> p n c", c=c), num_rows.rearrange("p (n c) -> p n c", c=c),
                        by_row(b["rd"][:, 0:n], c), ALU.mult).then_inc(S("divided"), 1)

    K = [ps[:, k, :] for k in range(8)]

    plan = {
        "gather_first": (0, "first_idx"), "load": (2, "pen_in"), "turn_x": (40, "xsT_ps xdT_ps"), "x_beta": (41, "xb xxb"),
        "gather": (68, "next_idx"), "copy_xT": (76, "xsT xdT"), "scores": (88, "z_ps zs_ps"), "copy_z": (116, "z zs"),
        "leaky": (129, "zl zsl zm"), "times_W": (145, "hs_ps hd_ps"), "maximum": (152, "M_first M dz Dm0 Dm dzs"),
        "exps": (190, "p F pself"), "sums": (221, "msg den num"), "self_part": (269, "self_msg den_self num_self"),
        "turn_sums": (292, "num_rows"), "divide": (359, "dn rd divided ob"), "gelu": (390, "gelu"),
        **ln_plan("a", 412, 428, 460, 468), "x1_pre": (547, "ag x1_pre"), **ln_plan("b", 597, 655, 662, 668),
        "turn_x1": (686, "x1T_ps"), "store_x1": (690, "x1_stored"), "copy_x1T": (698, "x1T"), "rows_xw": (705, "xw_ps"),
        "scale_xw": (805, "dis xw"), "store_xw": (815, "xw_stored")}
    new_phase()
    with ExitStack() as tmp:
        hop = Hop(tmp, "h0", plan, EL, HOP0_LAG, "xsT xdT pen z zs p F den num msg u v w x1 xw",
                  {"gs": (x, NT, src_idx), "gd": (x, NT, dst_idx)})
        B = hop.B

        def hop0_turn(it, new, old):
            with nc.Block() as block:
                @block.sync
                def _(sp):
                    step = hop.steps(it, new, old)

                    @step("load")
                    def _(L, i):
                        step.due_dma(sp, "x1_stored", L, EL)
                        step.due_dma(sp, "xw_stored", L, EL)
                        sp.dma_start(B[L]["pen"][:], hop.cols(pen_row, i, L)).then_inc(step.issue("pen_in", L), 16)

                    @step("store_x1")
                    def _(L, i):
                        step.due(sp, "b_out", L)
                        sp.dma_start(hop.rows(x1_slots, i, L, 0), rows4(B[L]["x1"][:])).then_inc(step.issue("x1_stored", L), 16)

                    @step("store_xw")
                    def _(L, i):
                        step.due(sp, "xw", L)
                        sp.dma_start(hop.rows(tables[0], i, L), rows4(B[L]["xw"][:])).then_inc(step.issue("xw_stored", L), 16)

                    step.run()
                    step.end_dmas(sp)

                @block.gpsimd
                def _(pool):
                    step = hop.steps(it, new, old)

                    @step("x_beta")
                    def _(L, i):
                        b = B[L]
                        step.due_dma(pool, "pen_in", L)
                        hop.due_gathered(pool, i, L)
                        nc.gpsimd.tensor_tensor(rows4(b["w"][:]), rows4(b["gd"][:]), each_row(beta0), ALU.add).then_inc(S("xb"), 1)
                        step.due(pool, "xb", L)
                        nc.gpsimd.tensor_tensor(b["w"][:], b["w"][:], b["gd"][:], ALU.add).then_inc(S("xxb"), 1)

                    hop.gather_steps(pool, step, ["xsT_ps", "xdT_ps", "xxb"])
                    step.run()
                    if not new:
                        hop.end_gathers(pool)

                @block.tensor
                def _(pe):
                    step = hop.steps(it, new, old)

                    @step("turn_x")
                    def _(L, i):
                        step.due_dma(pe, "pen_in", L)
                        step.due(pe, "z", L, 1)
                        hop.due_gathered(pe, i, L)
                        turn(pe, K[0], B[L]["gs"]).then_inc(S("xsT_ps"), 1)
                        step.due(pe, "zs", L, 1)
                        turn(pe, K[1], B[L]["gd"]).then_inc(S("xdT_ps"), 1)

                    @step("scores")
                    def _(L, i):
                        b = B[L]
                        step.due(pe, "xsT", L)
                        step.due(pe, "xdT", L)
                        nc.tensor.matmul(K[0], src_rep[:], b["xsT"][:], start=True, stop=False)
                        nc.tensor.matmul(K[0], dst_rep[:], b["xdT"][:], start=False, stop=True).then_inc(S("z_ps"), 1)
                        nc.tensor.matmul(K[1], self_rep[:], b["xdT"][:], start=True, stop=True).then_inc(S("zs_ps"), 1)

                    @step("times_W")
                    def _(L, i):
                        b = B[L]
                        step.due(pe, "msg", L, 1)
                        nc.tensor.matmul(K[2], W0[:], b["xsT"][:], start=True, stop=True).then_inc(S("hs_ps"), 1)
                        step.due(pe, "self_msg", L, 1)
                        nc.tensor.matmul(K[3], W0[:], b["xdT"][:], start=True, stop=True).then_inc(S("hd_ps"), 1)

                    @step("turn_sums")
                    def _(L, i):
                        b = B[L]
                        step.due(pe, "num_self", L)
                        step.due(pe, "den_self", L)
                        step.due(pe, "divided", L, 1)
                        turn(pe, K[4], b["u"])
                        den_rows(pe, K[5], b["v"], sel4, 4).then_inc(S("num_rows"), 1)

                    @step("turn_x1")
                    def _(L, i):
                        step.due(pe, "b_out", L)
                        step.due(pe, "x1T", L, 1)
                        turn(pe, K[6], B[L]["x1"]).then_inc(S("x1T_ps"), 1)

                    @step("rows_xw")
                    def _(L, i):
                        step.due(pe, "x1T", L)
                        step.due(pe, "xw", L, 1)
                        rows_times(pe, K[7], B[L]["xsT"], WI0, xw0_bias_row).then_inc(S("xw_ps"), 1)

                    step.run()

                @block.scalar
                def _(act):
                    step = hop.steps(it, new, old)

                    @step("copy_xT")
                    def _(L, i):
                        step.due(act, "xsT_ps", L)
                        nc.scalar.copy(B[L]["xsT"][:], K[0]).then_inc(S("xsT"), 1)
                        step.due(act, "xdT_ps", L)
                        nc.scalar.copy(B[L]["xdT"][:], K[1]).then_inc(S("xdT"), 1)

                    @step("copy_z")
                    def _(L, i):
                        b = B[L]
                        step.due(act, "z_ps", L)
                        nc.scalar.copy(b["z"][:], K[0]).then_inc(S("z"), 1)
                        step.due(act, "zs_ps", L)
                        nc.scalar.copy(b["zs"][:], K[1]).then_inc(S("zs"), 1)

                    @step("exps")
                    def _(L, i):
                        b = B[L]
                        run_weights(act, step, b, L)
                        step.due(act, "dzs", L)
                        nc.scalar.activation(b["zs"][:], b["zs"][:], ACT.Exp).then_inc(S("pself"), 1)

                    @step("gelu")
                    def _(L, i):
                        b = B[L]
                        step.due(act, "ob", L)
                        nc.scalar.activation(b["v"][:], b["msg"][:], ACT.Gelu).then_inc(S("gelu"), 1)

                    ln_act(act, step, B, "a", "u", "v")
                    ln_act(act, step, B, "b", "x1", "v")

                    @step("copy_x1T")
                    def _(L, i):
                        step.due(act, "x1T_ps", L)
                        nc.scalar.copy(B[L]["xsT"][:], K[6]).then_inc(S("x1T"), 1)

                    step.run()

                @block.vector
                def _(v):
                    V = nc.vector
                    step = hop.steps(it, new, old)
                    if step.first:
                        hop.no_sums(v, "M", "den", "num")

                    @step("leaky")
                    def _(L, i):
                        b = B[L]
                        step.due(v, "z", L)
                        V.scalar_tensor_tensor(out=b["z"][:], in0=b["z"][:], scalar=0.2, in1=b["z"][:], op0=ALU.mult, op1=ALU.max).then_inc(S("zl"), 1)
                        step.due(v, "zs", L)
                        V.scalar_tensor_tensor(out=b["zs"][:], in0=b["zs"][:], scalar=0.2, in1=b["zs"][:], op0=ALU.mult, op1=ALU.max).then_inc(S("zsl"), 1)
                        step.due(v, "zl", L)
                        step.due(v, "zsl", L)
                        V.tensor_tensor(b["u"][:], b["z"][:], b["zs"][:], ALU.max).then_inc(S("zm"), 1)

                    @step("maximum")
                    def _(L, i):
                        b = B[L]
                        run_maximum(v, step, hop, L, b["z"][:], b["u"][:], "zm")
                        V.tensor_tensor(b["zs"][:], b["zs"][:], b["M"][:, 1:CH + 1], ALU.subtract).then_inc(S("dzs"), 1)

                    @step("sums")
                    def _(L, i):
                        run_sums(v, step, hop, L, K[2], 0.0, "hs_ps")

                    @step("self_part")
                    def _(L, i):
                        b = B[L]
                        step.due(v, "pself", L)
                        step.due(v, "hd_ps", L)
                        V.tensor_tensor(b["z"][:], b["zs"][:], K[3], ALU.mult).then_inc(S("self_msg"), 1)
                        step.due(v, "den", L)
                        V.tensor_tensor(b["v"][:], b["den"][:], b["zs"][:], ALU.add).then_inc(S("den_self"), 1)
                        step.due(v, "self_msg", L)
                        step.due(v, "num", L)
                        V.tensor_tensor(b["u"][:], b["num"][:], b["z"][:], ALU.add).then_inc(S("num_self"), 1)

                    @step("divide")
                    def _(L, i):
                        b = B[L]
                        divide(v, step, b, L, K[4], K[5], 4, 1e-16, b["z"])
                        step.due(v, "divided", L)
                        V.tensor_tensor(rows4(b["msg"][:]), rows4(b["z"][:]), each_row(bias0), ALU.add).then_inc(S("ob"), 1)

                    ln_vector(v, step, B, "a", "v", "gelu")

                    @step("x1_pre")
                    def _(L, i):
                        b = B[L]
                        step.due(v, "a_out", L)
                        V.tensor_tensor(rows4(b["u"][:]), rows4(b["u"][:]), each_row(gamma0), ALU.mult).then_inc(S("ag"), 1)
                        step.due(v, "ag", L)
                        step.due(v, "xxb", L)
                        V.tensor_tensor(b["v"][:], b["u"][:], b["w"][:], ALU.add).then_inc(S("x1_pre"), 1)

                    ln_vector(v, step, B, "b", "v", "x1_pre")

                    @step("scale_xw")
                    def _(L, i):
                        b = B[L]
                        V.tensor_copy(b["dis"][:], dis[:, hop.tiles(i, L)]).then_inc(S("dis"), 1)
                        step.due(v, "xw_ps", L)
                        step.due(v, "dis", L)
                        V.tensor_tensor(rows4(b["xw"][:]), rows4(K[7]), by_row(b["dis"]), ALU.mult).then_inc(S("xw"), 1)

                    step.run()
            all_meet()

        turns(hop.n_it, hop0_turn)

    for layer in range(3):
        last_layer = layer == 2
        if last_layer:
            lag, plan = GCN_LAST_LAG, {
                "gather_first": (0, "first_idx"), "load": (1, "nst_in own_in x1_in"), "turn_x": (33, "xsT_ps"),
                "aggregate": (44, "agg"), "turn_agg": (54, "agg_rows"), "combine": (66, "dis with_self scaled h_pre"),
                "gather": (76, "next_idx"), "x2_pre": (89, "x2_pre"), **ln_plan("c", 104, 120, 138, 144), "store": (162, "stored")}
        else:
            lag, plan = GCN_LAG, {
                "gather_first": (0, "first_idx"), "load": (1, "nst_in own_in"), "turn_x": (32, "xsT_ps"), "gather": (44, "next_idx"),
                "aggregate": (57, "agg"), "turn_agg": (67, "agg_rows"), "combine": (78, "dis with_self scaled h_pre"),
                "turn_h": (100, "hT_ps"), "relu_h": (112, "hT"), "rows_xw": (131, "xw_ps"), "scale_xw": (155, "xw"), "store": (165, "stored")}
        new_phase()
        with ExitStack() as tmp:
            hop = Hop(tmp, f"g{layer}", plan, GL, lag, "own nst agg u " + ("x1 x2" if last_layer else "hT xw"),
                      {"gs": (tables[layer], NT + ET, slot_idx)}, maximum=False)
            B = hop.B
            new_rows, new_ready = ("x2", "c_out") if last_layer else ("xw", "xw")

            def gcn_turn(it, new, old):
                with nc.Block() as block:
                    @block.sync
                    def _(sp):
                        step = hop.steps(it, new, old)

                        @step("load")
                        def _(L, i):
                            b = B[L]
                            step.due_dma(sp, "stored", L, GL)
                            sp.dma_start(b["nst"][:], hop.cols(nst_row, i, L)).then_inc(step.issue("nst_in", L), 16)
                            sp.dma_start(rows4(b["own"][:]), hop.rows(tables[layer], i, L)).then_inc(step.issue("own_in", L), 16)
                            if last_layer:
                                sp.dma_start(rows4(b["x1"][:]), hop.rows(x1_slots, i, L, 0)).then_inc(step.issue("x1_in", L), 16)

                        @step("store")
                        def _(L, i):
                            step.due(sp, new_ready, L)
                            sp.dma_start(hop.rows(tables[layer + 1], i, L), rows4(B[L][new_rows][:])).then_inc(step.issue("stored", L), 16)

                        step.run()
                        step.end_dmas(sp)

                    @block.gpsimd
                    def _(pool):
                        step = hop.steps(it, new, old)
                        hop.gather_steps(pool, step, ["xsT_ps"])
                        step.run()
                        if not new:
                            hop.end_gathers(pool)

                    @block.tensor
                    def _(pe):
                        step = hop.steps(it, new, old)

                        @step("turn_x")
                        def _(L, i):
                            step.due(pe, "agg", L, 1)
                            hop.due_gathered(pe, i, L)
                            turn(pe, K[0], B[L]["gs"]).then_inc(S("xsT_ps"), 1)

                        @step("turn_agg")
                        def _(L, i):
                            step.due(pe, "agg", L)
                            step.due(pe, "with_self", L, 1)
                            turn(pe, K[1], B[L]["agg"]).then_inc(S("agg_rows"), 1)

                        if not last_layer:
                            @step("turn_h")
                            def _(L, i):
                                step.due(pe, "h_pre", L)
                                step.due(pe, "hT", L, 1)
                                turn(pe, K[2], B[L]["u"]).then_inc(S("hT_ps"), 1)

                            @step("rows_xw")
                            def _(L, i):
                                step.due(pe, "hT", L)
                                step.due(pe, "xw", L, 1)
                                rows_times(pe, K[3], B[L]["hT"], WS[layer + 1]).then_inc(S("xw_ps"), 1)

                        step.run()

                    @block.scalar
                    def _(act):
                        step = hop.steps(it, new, old)
                        if last_layer:
                            ln_act(act, step, B, "c", "x2", "u")
                        else:
                            @step("relu_h")
                            def _(L, i):
                                step.due(act, "hT_ps", L)
                                nc.scalar.activation(B[L]["hT"][:], K[2], ACT.Relu).then_inc(S("hT"), 1)
                        step.run()

                    @block.vector
                    def _(v):
                        V = nc.vector
                        step = hop.steps(it, new, old)
                        if step.first:
                            hop.no_sums(v, "agg")

                        @step("aggregate")
                        def _(L, i):
                            b = B[L]
                            step.due(v, "xsT_ps", L)
                            step.due_dma(v, "nst_in", L)
                            step.due(v, "agg", L, 1)
                            V.tensor_tensor_scan(b["agg"][:], b["nst"][:], K[0], hop.before(L)["agg"][:, CH - 1:CH], ALU.mult, ALU.add).then_inc(S("agg"), 1)

                        @step("combine")
                        def _(L, i):
                            b = B[L]
                            V.tensor_copy(b["dis"][:], dis[:, hop.tiles(i, L)]).then_inc(S("dis"), 1)
                            step.due(v, "agg_rows", L)
                            step.due_dma(v, "own_in", L)
                            V.tensor_tensor(b["u"][:], K[1], b["own"][:], ALU.add).then_inc(S("with_self"), 1)
                            step.due(v, "with_self", L)
                            step.due(v, "dis", L)
                            V.tensor_tensor(rows4(b["u"][:]), rows4(b["u"][:]), by_row(b["dis"]), ALU.mult).then_inc(S("scaled"), 1)
                            step.due(v, "scaled", L)
                            V.tensor_tensor(rows4(b["u"][:]), rows4(b["u"][:]), each_row(bs_row[layer]), ALU.add).then_inc(S("h_pre"), 1)

                        if last_layer:
                            @step("x2_pre")
                            def _(L, i):
                                b = B[L]
                                step.due(v, "h_pre", L)
                                step.due_dma(v, "x1_in", L)
                                V.scalar_tensor_tensor(out=b["u"][:], in0=b["u"][:], scalar=0.0, in1=b["x1"][:],
                                                       op0=ALU.max, op1=ALU.add).then_inc(S("x2_pre"), 1)

                            ln_vector(v, step, B, "c", "u", "x2_pre")
                        else:
                            @step("scale_xw")
                            def _(L, i):
                                b = B[L]
                                step.due(v, "xw_ps", L)
                                V.tensor_tensor(rows4(b["xw"][:]), rows4(K[3]), by_row(b["dis"]), ALU.mult).then_inc(S("xw"), 1)
                        step.run()
                all_meet()

            turns(hop.n_it, gcn_turn)

    for kind in (2, 3):
        heads = 8 if kind == 2 else 4
        width = 32 if kind == 2 else 64
        table, ea = tables[kind + 1], (ea32 if kind == 2 else ea64)
        if kind == 2:
            lag, plan = HOP4_LAG, {
                "gather_first": (0, "first_idx"), "load": (1, "ea_in pen_in"), "residual": (30, "xo x2b"),
                "turn_x": (38, "xsT_ps xdT_ps eaT_ps"), "copy_xT": (66, "xsT xdT eaT"), "products": (84, "k_ps q_ps"),
                "values": (101, "v_ps"), "copy_z": (112, "kb"), "qk": (120, "qk"), "scores": (129, "z_ps"),
                "maximum": (149, "M_first M dz Dm0 Dm"), "gather": (169, "next_idx"), "exps": (181, "p F"),
                "sums": (232, "msg den num"), "turn_sums": (255, "num_rows"), "divide": (270, "dn rd divided"),
                "turn_o": (285, "oT_ps"), "copy_oT": (296, "oT"), "rows_o": (304, "wo_ps"), "h_res": (317, "h_res"),
                **ln_plan("d", 326, 394, 419, 439), "x3_pre": (478, "dg x3_pre"), **ln_plan("e", 494, 510, 528, 547),
                "store": (565, "stored")}
        else:
            lag, plan = HOP5_LAG, {
                "gather_first": (0, "first_idx"), "load": (1, "ea_in pen_in ew_in"), 
                "turn_x": (72, "xsT_ps xdT_ps eaT_ps"), "copy_xT": (100, "xsT xdT eaT"), "residual": (105, "xo"), "products": (136, "z_ps"),
                "gather": (159, "next_idx"), "values": (163, "v_ps"), "copy_z": (174, "kb"), "qk": (218, "zl"),
                "maximum": (227, "M_first M dz Dm0 Dm"), "exps": (261, "p F"), "sums": (286, "msg den num"),
                "turn_sums": (342, "num_rows"), "divide": (403, "dn rd divided"), "x4_pre": (416, "x4_pre"),
                **ln_plan("f", 474, 490, 516, 522), "scatter": (540, "end_now"), "scattered": (685, "x4_free")}
        new_phase()
        with ExitStack() as tmp:
            hop = Hop(tmp, f"t{kind}", plan, EL, lag, "xsT xdT pen kb qk p F den num msg xo " + ("w" if kind == 2 else "u x4"),
                      {"gs": (table, NT + ET, slot_idx), "own": (table, NT + ET, own_idx)})
            B = hop.B
            for L, b in enumerate(B):
                b["ea"] = tmp.enter_context(nc.sbuf_tensor(f"ea_{kind}_{L}", [P, SUB * width], F32))
                b["eaT"] = tmp.enter_context(nc.sbuf_tensor(f"eaT_{kind}_{L}", [width + 1, CH], F32))
                if kind == 2:
                    b["o"], b["u"], b["v"], b["xn"] = b["kb"], b["F"], b["p"], b["msg"]
                else:
                    b["o"] = b["kb"]
                    b["end_now"] = tmp.enter_context(nc.sbuf_tensor(f"end_now_{L}", [P, SUB], U32))
            flag = tmp.enter_context(nc.sbuf_tensor(f"flag{kind}", [1, EL], F32))

            def attention_turn(it, new, old):
                with nc.Block() as block:
                    @block.sync
                    def _(sp):
                        step = hop.steps(it, new, old)

                        @step("load")
                        def _(L, i):
                            b = B[L]
                            if kind == 2:
                                step.due_dma(sp, "stored", L, EL)
                            else:
                                step.due(sp, "f_out", L, EL)
                            sp.dma_start(b["ea"].rearrange("p (j f) -> p j f", j=SUB), hop.rows(ea, i, L, 0)).then_inc(step.issue("ea_in", L), 16)
                            sp.dma_start(b["pen"][:], hop.cols(pen_row, i, L)).then_inc(step.issue("pen_in", L), 16)
                            if kind == 3:
                                sp.dma_start(b["eaT"][64:65, :], hop.cols(ew, i, L, 1)).then_inc(step.issue("ew_in", L), 16)

                        if kind == 2:
                            @step("store")
                            def _(L, i):
                                step.due(sp, "e_out", L)
                                sp.dma_start(hop.rows(tables[4], i, L), rows4(B[L]["xn"][:])).then_inc(step.issue("stored", L), 16)

                        step.run()
                        step.end_dmas(sp)

                    @block.gpsimd
                    def _(pool):
                        step = hop.steps(it, new, old)

                        if kind == 2:
                            @step("residual")
                            def _(L, i):
                                b = B[L]
                                step.due_dma(pool, "ea_in", L)
                                hop.due_gathered(pool, i, L)
                                nc.gpsimd.tensor_tensor(rows4(b["xo"][:]), rows4(b["own"][:]), each_row(bo), ALU.add).then_inc(S("xo"), 1)
                                nc.gpsimd.tensor_tensor(rows4(b["w"][:]), rows4(b["own"][:]), each_row(beta2), ALU.add).then_inc(S("x2b"), 1)

                        hop.gather_steps(pool, step, ["xsT_ps", "xdT_ps", "xo"] + ["x2b"] * (kind == 2))

                        if kind == 3:
                            @step("scatter")
                            def _(L, i):
                                b = B[L]
                                nc.gpsimd.tensor_copy(b["end_now"][:], end_idx[:, hop.tiles(i, L)]).then_inc(S("end_now"), 1)
                                step.due(pool, "end_now", L)
                                step.due(pool, "f_out", L)
                                for t in range(SUB):
                                    pool.indirect_dma_start(out=out, out_offset=bass.IndirectOffsetOnAxis(ap=b["end_now"][:, t:t + 1], axis=0),
                                                            in_=b["x4"][:, t * D:(t + 1) * D], in_offset=None,
                                                            bounds_check=NODES - 1, oob_is_err=False).then_inc(pool_dma[f"scattered{L}"], 16)

                            @step("scattered")
                            def _(L, i):
                                pool.wait_ge(pool_dma[f"scattered{L}"], (i + 1) * (16 * SUB))
                                nc.gpsimd.tensor_tensor(flag[:, L:L + 1], eps[0:1, :], eps[0:1, :], ALU.add).then_inc(S("x4_free"), 1)

                        step.run()
                        if not new:
                            hop.end_gathers(pool)

                    @block.tensor
                    def _(pe):
                        step = hop.steps(it, new, old)
                        if step.first and kind == 2:
                            pe.wait_ge(S("be_row"), EL)

                        @step("turn_x")
                        def _(L, i):
                            b = B[L]
                            step.due_dma(pe, "ea_in", L)
                            step.due(pe, "kb" if kind == 2 else "xsT", L, 1)
                            hop.due_gathered(pe, i, L)
                            turn(pe, K[0], b["gs"]).then_inc(S("xsT_ps"), 1)
                            step.due(pe, "qk" if kind == 2 else "kb", L, 1)
                            turn(pe, K[1], b["own"]).then_inc(S("xdT_ps"), 1)
                            step.due(pe, "M" if kind == 2 else "eaT", L, 1)
                            if kind == 2:
                                step.due(pe, "dz", L, 1)
                            turn(pe, K[2], b["ea"], width).then_inc(S("eaT_ps"), 1)

                        @step("products")
                        def _(L, i):
                            b = B[L]
                            step.due(pe, "xsT", L)
                            step.due(pe, "xdT", L)
                            if kind == 2:
                                nc.tensor.matmul(K[0], Wk[:], b["xsT"][:], start=True, stop=True).then_inc(S("k_ps"), 1)
                                nc.tensor.matmul(K[1], Wq[:], b["xdT"][:], start=True, stop=True).then_inc(S("q_ps"), 1)
                            else:
                                step.due(pe, "eaT", L)
                                step.due_dma(pe, "ew_in", L)
                                nc.tensor.matmul(K[1], k3_rep[:], b["xsT"][:], start=True, stop=False)
                                nc.tensor.matmul(K[1], q3_rep[:], b["xdT"][:], start=False, stop=False)
                                nc.tensor.matmul(K[1], we3_rep[:], b["eaT"][:], start=False, stop=True).then_inc(S("z_ps"), 1)

                        @step("values")
                        def _(L, i):
                            step.due(pe, "msg", L, 1)
                            nc.tensor.matmul(K[3], (Wv if kind == 2 else Wv3)[:], B[L]["xsT"][:], start=True, stop=True).then_inc(S("v_ps"), 1)

                        if kind == 2:
                            @step("scores")
                            def _(L, i):
                                b = B[L]
                                step.due(pe, "eaT", L)
                                nc.tensor.matmul(K[2], we2_rep[:], b["eaT"][:], start=True, stop=False)
                                step.due(pe, "qk", L)
                                nc.tensor.matmul(K[2], head_sum[:], b["qk"][:], start=False, stop=True).then_inc(S("z_ps"), 1)

                            @step("turn_o")
                            def _(L, i):
                                step.due(pe, "divided", L)
                                step.due(pe, "oT", L, 1)
                                turn(pe, K[6], B[L]["o"]).then_inc(S("oT_ps"), 1)

                            @step("rows_o")
                            def _(L, i):
                                step.due(pe, "oT", L)
                                step.due(pe, "h_res", L, 1)
                                rows_times(pe, K[7], B[L]["xsT"], Wo).then_inc(S("wo_ps"), 1)

                        @step("turn_sums")
                        def _(L, i):
                            b = B[L]
                            step.due(pe, "num", L)
                            step.due(pe, "divided", L, 1)
                            turn(pe, K[4], b["num"])
                            den_rows(pe, K[5], b["den"], sel8 if kind == 2 else sel4, heads).then_inc(S("num_rows"), 1)

                        step.run()

                    @block.scalar
                    def _(act):
                        step = hop.steps(it, new, old)

                        @step("copy_xT")
                        def _(L, i):
                            b = B[L]
                            step.due(act, "xsT_ps", L)
                            nc.scalar.copy(b["xsT"][:], K[0]).then_inc(S("xsT"), 1)
                            step.due(act, "xdT_ps", L)
                            nc.scalar.copy(b["xdT"][:], K[1]).then_inc(S("xdT"), 1)
                            step.due(act, "eaT_ps", L)
                            nc.scalar.copy(b["eaT"][0:width, :], K[2][0:width, :]).then_inc(S("eaT"), 1)

                        @step("copy_z")
                        def _(L, i):
                            b = B[L]
                            if kind == 2:
                                step.due(act, "k_ps", L)
                                nc.scalar.activation(b["kb"][:], K[0], ACT.Identity, bias=bk[:, 0:1]).then_inc(S("kb"), 1)
                            else:
                                step.due(act, "z_ps", L)
                                nc.scalar.mul(b["kb"][:], K[1], float(32.0 ** -0.5)).then_inc(S("kb"), 1)

                        @step("exps")
                        def _(L, i):
                            run_weights(act, step, B[L], L)

                        if kind == 2:
                            @step("copy_oT")
                            def _(L, i):
                                step.due(act, "oT_ps", L)
                                nc.scalar.copy(B[L]["xsT"][:], K[6]).then_inc(S("oT"), 1)

                            ln_act(act, step, B, "d", "v", "u")
                            ln_act(act, step, B, "e", "xn", "u")
                        else:
                            @step("f.root")
                            def _(L, i):
                                ln_root(act, step, "f", L, B[L])

                            @step("f.apply")
                            def _(L, i):
                                step.due(act, "x4_free", L, EL)
                                ln_apply(act, step, "f", L, B[L], B[L]["x4"], B[L]["u"])

                        step.run()

                    @block.vector
                    def _(v):
                        V = nc.vector
                        step = hop.steps(it, new, old)
                        if step.first:
                            if kind == 2:
                                for b in B:
                                    V.memset(b["eaT"][width:width + 1, :], 1.0).then_inc(S("be_row"), 1)
                            hop.no_sums(v, "M", "den", "num")

                        @step("qk")
                        def _(L, i):
                            b = B[L]
                            step.due(v, "kb", L)
                            if kind == 2:
                                step.due(v, "q_ps", L)
                                V.scalar_tensor_tensor(out=b["qk"][:], in0=K[1], scalar=bq[:, 0:1], in1=b["kb"][:],
                                                       op0=ALU.add, op1=ALU.mult).then_inc(S("qk"), 1)
                            else:
                                V.scalar_tensor_tensor(out=b["qk"][:], in0=b["kb"][:], scalar=0.2, in1=b["kb"][:],
                                                       op0=ALU.mult, op1=ALU.max).then_inc(S("zl"), 1)

                        @step("maximum")
                        def _(L, i):
                            score = K[2] if kind == 2 else B[L]["qk"][:]
                            run_maximum(v, step, hop, L, score, score, "z_ps" if kind == 2 else "zl")

                        @step("sums")
                        def _(L, i):
                            run_sums(v, step, hop, L, K[3], bv[:, 0:1] if kind == 2 else 0.0, "v_ps")

                        @step("divide")
                        def _(L, i):
                            b = B[L]
                            divide(v, step, b, L, K[4], K[5], heads, 1e-8 if kind == 2 else 1e-16, b["o"])

                        if kind == 2:
                            @step("h_res")
                            def _(L, i):
                                b = B[L]
                                step.due(v, "wo_ps", L)
                                step.due(v, "xo", L)
                                V.tensor_tensor(b["u"][:], K[7], b["xo"][:], ALU.add).then_inc(S("h_res"), 1)

                            ln_vector(v, step, B, "d", "u", "h_res")

                            @step("x3_pre")
                            def _(L, i):
                                b = B[L]
                                step.due(v, "d_out", L)
                                V.tensor_tensor(rows4(b["v"][:]), rows4(b["v"][:]), each_row(gamma2), ALU.mult).then_inc(S("dg"), 1)
                                step.due(v, "dg", L)
                                step.due(v, "x2b", L)
                                V.tensor_tensor(b["u"][:], b["v"][:], b["w"][:], ALU.add).then_inc(S("x3_pre"), 1)

                            ln_vector(v, step, B, "e", "u", "x3_pre")
                        else:
                            @step("residual")
                            def _(L, i):
                                b = B[L]
                                step.due(v, "xdT_ps", L)
                                V.tensor_tensor(rows4(b["xo"][:]), rows4(b["own"][:]), each_row(bias3), ALU.add).then_inc(S("xo"), 1)

                            @step("x4_pre")
                            def _(L, i):
                                b = B[L]
                                step.due(v, "divided", L)
                                step.due(v, "xo", L)
                                V.tensor_tensor(b["u"][:], b["o"][:], b["xo"][:], ALU.add).then_inc(S("x4_pre"), 1)

                            ln_vector(v, step, B, "f", "u", "x4_pre")

                        step.run()
                all_meet()

            turns(hop.n_it, attention_turn)
    ctx.close()


def kernel(**inputs):
    import numpy as np
    from concourse import bacc
    from concourse.bass_utils import run_bass_kernel_spmd

    def padded(a, n, value=0):
        a = np.ascontiguousarray(a)
        return np.concatenate([a, np.full((n - a.shape[0],) + a.shape[1:], value, a.dtype)])

    dst = np.asarray(inputs["dst"])
    arrays = {
        "x": padded(inputs["x"], NT),
        "src": padded(inputs["src"], ET),
        "dst": padded(np.concatenate([np.full((1,), -1, dst.dtype), dst]), ET + 2, NODES),
        "ea32": padded(inputs["edge_attr_32"], ET),
        "ea64": padded(inputs["edge_attr_64"], ET),
        "ew": padded(inputs["edge_weight"], ET).reshape(1, ET),
    }
    weights = {k: np.ascontiguousarray(v) for k, v in inputs.items() if k.startswith("L")}
    nc = bacc.Bacc("TRN2", target_bir_lowering=False, num_devices=1)

    def declare(name, a):
        return nc.dram_tensor(name, list(a.shape), mybir.dt.from_np(a.dtype), kind="ExternalInput").ap()

    edge = [declare(n, a) for n, a in arrays.items()]
    w = {n: declare(n, a) for n, a in weights.items()}
    out = nc.dram_tensor("out", [NT, D], F32, kind="ExternalOutput").ap()
    build(nc, *edge, w, out)
    r = run_bass_kernel_spmd(nc, [{**arrays, **weights}], core_ids=[0])
    return r.results[0]["out"][:NODES]
```
